# Optimizing a Trainium2 kernel written in Bass

```python
import numpy as np
import jax
import jax.numpy as jnp

def _softmax(x, axis=-1):
    return jax.nn.softmax(x, axis=axis)

def _gelu(x):
    return jax.nn.gelu(x, approximate=True)

def _silu(x):
    return jax.nn.silu(x)

def _sigmoid(x):
    return jax.nn.sigmoid(x)

def _layernorm(x, axis=-1, eps=1e-05):
    m = jnp.mean(x, axis=axis, keepdims=True)
    v = jnp.var(x, axis=axis, keepdims=True)
    return (x - m) / jnp.sqrt(v + eps)

def _scatter_add(tgt, idx, src, axis=0):
    return tgt.at[idx].add(src)

def _segment_sum(src, seg, n):
    return jax.ops.segment_sum(src, seg, n)
kernel_name = 'mk_gnn_resnorm_d1_gnn_r64_fb4d2c'

def setup_inputs(seed: int=0):
    np.random.seed(seed)
    _w = jnp.asarray

    def _rec_inputs():
        import jax
        import jax.numpy as jnp
        _gk = jax.random.key(seed)
        x = -8.776e-05 + 1 * jax.random.normal(jax.random.fold_in(_gk, 1), (50000, 512), jnp.float32)
        _s = jax.random.randint(jax.random.fold_in(_gk, 2), (6250,), 0, 50000, jnp.int32)
        _d = jax.random.randint(jax.random.fold_in(_gk, 3), (6250,), 0, 50000, jnp.int32)
        _loop = jnp.arange(50000, dtype=jnp.int32)
        src = jnp.concatenate([_s, _d, _loop])
        dst = jnp.concatenate([_d, _s, _loop])
        _o = jnp.argsort(dst, stable=True)
        src = src[_o]
        dst = dst[_o]
        return (x, src, dst)
    x, src, dst = _rec_inputs()

    def _L0_gnn_setup():
        import jax, jax.numpy as jnp
        import numpy as np
        N_NODES = 10000
        N_EDGES = 2500
        D_IN = 512
        D_OUT = 512
        key = jax.random.key(seed)
        k_x, k_e, k_wl, k_wr = jax.random.split(key, 4)
        x = jax.random.normal(k_x, (N_NODES, D_IN), dtype=jnp.float32)
        edge_index = jax.random.randint(k_e, (2, N_EDGES), 0, N_NODES, dtype=jnp.int64)
        scale = 1.0 / np.sqrt(D_IN)
        W_l = jax.random.normal(k_wl, (D_IN, D_OUT), dtype=jnp.float32) * scale
        W_r = jax.random.normal(k_wr, (D_IN, D_OUT), dtype=jnp.float32) * scale
        b = jnp.zeros((D_OUT,), dtype=jnp.float32)
        return {'x': x, 'edge_index': edge_index, 'W_l': W_l, 'W_r': W_r, 'b': b}
    _L0_gnn_all = _L0_gnn_setup()
    _L0_gnn_in = {k: v for k, v in _L0_gnn_all.items() if k in ('W_l', 'W_r', 'b')}
    del _L0_gnn_all
    return {'x': x, 'src': src, 'dst': dst, 'L0_gnn_W_l': _L0_gnn_in['W_l'], 'L0_gnn_W_r': _L0_gnn_in['W_r'], 'L0_gnn_b': _L0_gnn_in['b']}

def reference(x, src, dst, L0_gnn_W_l, L0_gnn_W_r, L0_gnn_b):
    import jax
    import jax.numpy as jnp

    def _L0_gnn_ref(x, edge_index, W_l, W_r, b):
        import jax, jax.numpy as jnp
        import numpy as np
        N_NODES = 10000
        N_EDGES = 2500
        D_IN = 512
        D_OUT = 512
        src = edge_index[0]
        dst = edge_index[1]
        n = x.shape[0]
        msg = x[src]
        agg = jax.ops.segment_sum(msg, dst, num_segments=n)
        deg = jax.ops.segment_sum(jnp.ones((src.shape[0],), x.dtype), dst, num_segments=n)
        mean = agg / jnp.maximum(deg, 1.0)[:, None]
        h = mean @ W_l + b + x @ W_r
        return h * jax.nn.sigmoid(h)
    edge_index = jnp.stack([src, dst])
    x = _layernorm(x + _L0_gnn_ref(x, edge_index, L0_gnn_W_l, L0_gnn_W_r, L0_gnn_b), axis=-1)
    return x

_drawn_inputs = setup_inputs


def setup_inputs(seed=0):
    import zlib

    import numpy as np

    out = dict(_drawn_inputs(seed))
    spreads = {'L0_gnn_b': (0.0, 0.1)}
    factors = {}
    for name, (base, spread) in spreads.items():
        noise = np.random.default_rng([zlib.crc32(name.encode()), seed]).standard_normal(out[name].shape)
        drawn = base * np.exp(spread * noise) if base else spread * noise
        out[name] = jnp.asarray(drawn.astype(out[name].dtype))
    for name, factor in factors.items():
        out[name] = (out[name] * factor).astype(out[name].dtype)
    return out
```

```python
from contextlib import ExitStack

import concourse.bass as bass
from concourse import mybir


def gnn_layer(nc, x, src, dst, w_l, w_r, bias, out):
    f32, f32r, i32 = mybir.dt.float32, mybir.dt.float32r, mybir.dt.int32
    ALU = mybir.AluOpType
    ACT = mybir.ActivationFunctionType
    P = nc.NUM_PARTITIONS

    N, D = x.shape
    E = src.shape[0]
    R = E - N
    K = D // P
    EPS = 1e-5

    EDGE_ROWS, EDGE_TAIL = E // P, E % P
    CH = -(-(EDGE_ROWS + 1) // P)
    FULL = (CH - 1) * P
    COLS = CH * P
    ROW_BITS = P.bit_length() - 1
    BITS = (N - 1).bit_length()
    ET = -(-R // P)
    R_LAST = R - (ET - 1) * P
    NTILES = -(-N // P)
    N_LAST = N - (NTILES - 1) * P
    NP = -(-NTILES // 2)
    SKIP = 1 << 20
    assert NTILES % 2 == 1 and ET % 2 == 0 and NP % 4 == 0 and COLS <= 512
    assert BITS - ROW_BITS <= COLS.bit_length()

    corr = nc.dram_tensor("correction_rows", (ET * P, D), f32, kind="Internal").ap()
    src_rows = src.rearrange("(e a) -> e a", a=1)

    ctx = ExitStack()
    with ctx:
        def sb(name, shape, dt):
            return ctx.enter_context(nc.sbuf_tensor(name, shape, dt))

        def sem(name):
            return ctx.enter_context(nc.semaphore(name))

        eye3 = sb("eye3", [P, 3 * P], f32)
        eye = eye3[:, P:2 * P]
        ones = sb("ones", [P, P], f32)
        zeros = sb("zeros", [P, P], f32)
        minus_half = sb("minus_half", [P, 2], f32)
        bias_rows = sb("bias_rows", [P, D], f32)
        wl_raw = sb("wl_raw", [P, K, D], f32)
        wr_raw = sb("wr_raw", [P, K, D], f32)
        w_sum = sb("w_sum", [P, K, D], f32)
        ws_hi, ws_lo = sb("ws_hi", [P, K, D], f32r), sb("ws_lo", [P, K, D], f32r)
        wl_hi, wl_lo = sb("wl_hi", [P, K, D], f32r), sb("wl_lo", [P, K, D], f32r)
        X = sb("X", [P, 4, 2, D], f32)
        x_hi = [sb(f"x_hi{b}", [P, 2, K, P], f32r) for b in range(2)]
        x_lo = [sb(f"x_lo{b}", [P, 2, K, P], f32r) for b in range(2)]
        cor = [sb(f"cor{b}", [P, 2, D], f32) for b in range(4)]
        Z = sb("Z", [P, 2, 2, D], f32)
        O = sb("O", [P, 2, 2, D], f32)
        stats = sb("stats", [P, 2, 2, nc.vector.BN_STATS_DIM], f32)
        mv = sb("mv", [P, 2, 2, 2], f32)
        var_eps = sb("var_eps", [P, 2, 2], f32)
        rstd = sb("rstd", [P, 2, 2], f32)
        shift = sb("shift", [P, 2, 2], f32)
        node_idx = sb("node_idx", [P, NTILES + 1], i32)
        node_now = [sb(f"node_now{b}", [P, 2], i32) for b in range(4)]
        edge_idx = sb("edge_idx", [P, ET], i32)
        dst_idx = sb("dst_idx", [P, ET], i32)
        dst_f = sb("dst_f", [P, 1 + ET], f32)
        rdeg = sb("rdeg", [P, ET], f32)
        edge_now = [sb(f"edge_now{b}", [P, 1], i32) for b in range(2)]
        dst_now = [sb(f"dst_now{b}", [P, 1], i32) for b in range(2)]
        src_now = [sb(f"src_now{b}", [P, 1], i32) for b in range(2)]
        xs = [sb(f"xs{b}", [P, D], f32) for b in range(2)]
        xd = [sb(f"xd{b}", [P, D], f32) for b in range(2)]
        diff = [sb(f"diff{b}", [P, D], f32) for b in range(2)]
        dst_wide = [sb(f"dst_wide{b}", [P, P], f32) for b in range(2)]
        dst_row = sb("dst_row", [P, 2, 1 + P], f32)
        same = [sb(f"same{b}", [P, P], f32) for b in range(2)]
        goes_on = sb("goes_on", [P, 2, P], f32)
        sums = sb("sums", [P, 2, K, P], f32)
        s_hi = [sb(f"s_hi{b}", [P, K, P], f32r) for b in range(2)]
        s_lo = [sb(f"s_lo{b}", [P, K, P], f32r) for b in range(2)]
        c_out = sb("c_out", [P, 2, D], f32)
        Xi = X[:].bitcast(i32)
        rowed = [Xi[:, 2 * b:2 * b + 2].rearrange("p a t (c j) -> p (a t c) j", j=2 * P) for b in range(2)]
        assert 2 * CH * 2 * P <= 2 * 2 * D
        row_mask = sb("row_mask", [P, 2 * CH, 2 * P], i32)
        rowed_f = sb("rowed_f", [P, 2 * CH, 2 * P], f32)
        col = [cor[b][:].bitcast(i32) for b in range(2)]
        col_mask = cor[2][:].bitcast(i32)
        e_dst = cor[3][:, 0].bitcast(i32).rearrange("p (c j) -> p c j", j=P)
        e_next = cor[3][:, 1].bitcast(i32).rearrange("p (c j) -> p c j", j=P)
        e_pos = Z[:, 0, 0].bitcast(i32).rearrange("p (c j) -> p c j", j=P)
        e_other = Z[:, 0, 1].bitcast(i32).rearrange("p (c j) -> p c j", j=P)
        e_loop = Z[:, 1, 0].bitcast(i32).rearrange("p (c j) -> p c j", j=P)
        e_rank = Z[:, 1, 1].bitcast(i32).rearrange("p (c j) -> p c j", j=P)
        upto = O[:, 0, 0, 0:1 + NTILES]
        none = O[:, 0, 1, 0:NTILES]
        r_pos = O[:, 1, 0, 0:ET].bitcast(i32)
        dst_c = O[:, 1, 0, P:P + ET].bitcast(i32)
        t_dst = O[:, 1, 1, 0:1 + P]
        t_same = O[:, 1, 1, P + 16:P + 16 + P]
        t_run = sums[:, 0, 0]
        t_whole = sums[:, 0, 1]
        t_count = sums[:, 0, 2]
        t_rdeg = sums[:, 0, 3]
        row_ends = sb("row_ends", [1, 3, P], f32)

        pT = [ctx.enter_context(nc.psum_tensor(f"pT{b}", [P, 2, D], f32)) for b in range(2)]
        pH = [ctx.enter_context(nc.psum_tensor(f"pH{b}", [P, 2, D], f32)) for b in range(2)]

        pads_zero, edges_in, bias_in, weights_in = sem("pads_zero"), sem("edges_in"), sem("bias_in"), sem("weights_in")
        eye_clear, consts, pos_made = sem("eye_clear"), sem("consts"), sem("pos_made")
        w_summed, w_rounded, w_split = sem("w_summed"), sem("w_rounded"), sem("w_split")
        dve_step, rows_moved, merged = sem("dve_step"), sem("rows_moved"), sem("merged")
        dst_padded, dst_ready, dst_found = sem("dst_padded"), sem("dst_ready"), sem("dst_found")
        upto_ready, before_ready = sem("upto_ready"), sem("before_ready")
        t_ready, t_scanned, ends_ready, ends_copied = sem("t_ready"), sem("t_scanned"), sem("ends_ready"), sem("ends_copied")
        carry_ready, carry_col, t_deg, rdeg_ps, rdeg_ready = (sem("carry_ready"), sem("carry_col"), sem("t_deg"),
                                                             sem("rdeg_ps"), sem("rdeg_ready"))
        idx_ready = sem("idx_ready")
        gate, dve_gate = sem("gate"), sem("dve_gate")
        now_copied = sem("now_copied")
        src_in = [sem(f"src_in{b}") for b in range(2)]
        xs_in = [sem(f"xs_in{b}") for b in range(2)]
        xd_in = [sem(f"xd_in{b}") for b in range(2)]
        wide_made, row_made, row_kept, sames_made, diff_made = (sem("wide_made"), sem("row_made"), sem("row_kept"),
                                                               sem("sames_made"), sem("diff_made"))
        summed, sums_made, s_hi_made, s_lo_made, c_product, c_made = (sem("summed"), sem("sums_made"),
                                                                     sem("s_hi_made"), sem("s_lo_made"),
                                                                     sem("c_product"), sem("c_made"))
        c_stored = [sem(f"c_stored{b}") for b in range(2)]
        x_in = [sem(f"x_in{b}") for b in range(4)]
        cor_in = [sem(f"cor_in{b}") for b in range(4)]
        transposed, hi_made, lo_made, product, z_made, silu_made = (sem("transposed"), sem("hi_made"), sem("lo_made"),
                                                                   sem("product"), sem("z_made"), sem("silu_made"))
        u_made, stats_made, mv_made, eps_added, rstd_made, shift_made, normed = (
            sem("u_made"), sem("stats_made"), sem("mv_made"), sem("eps_added"), sem("rstd_made"),
            sem("shift_made"), sem("normed"))
        cor_reset = sem("cor_reset")
        stored = [sem(f"stored{b}") for b in range(2)]

        block = ctx.enter_context(nc.Block())

        def fixed(v):
            return isinstance(v, int)

        def wait(eng, s, v):
            if not fixed(v) or v > 0:
                eng.wait_ge(s, v)

        def steps(eng, n, unroll, head, tail, step):
            rounds = n // unroll
            for q in range(head):
                for u in range(unroll):
                    step(q * unroll + u, q, u)
            with eng.Fori(head, rounds - tail) as q:
                for u in range(unroll):
                    step(q * unroll + u, q, u)
            for q in range(rounds - tail, rounds):
                for u in range(unroll):
                    step(q * unroll + u, q, u)

        def edge_steps(eng, step):
            steps(eng, ET, 2, 1, 2, step)

        def pair_steps(eng, step):
            steps(eng, NP, 4, 1, 1, step)

        def there(t, n):
            return not fixed(t) or 0 <= t < n

        def ring(q, u, off, unroll, n):
            return (u + off) % n, q * (unroll // n) + (u + off) // n

        def pair_shape(j):
            return (1, N_LAST) if fixed(j) and j == NP - 1 else (2, P)

        @block.sync
        def _(sp):
            sp.wait_ge(pads_zero, 2)
            for tile, first in ((e_dst, 0), (e_next, 1)):
                sp.dma_start(tile[:, 0:CH - 1], dst[first:first + FULL * P].rearrange("(c p j) -> p c j", p=P, j=P)
                             ).then_inc(edges_in, 16)
                rows = EDGE_ROWS - FULL
                sp.dma_start(tile[0:rows, CH - 1], dst[first + FULL * P:first + EDGE_ROWS * P]
                             .rearrange("(p j) -> p j", j=P)).then_inc(edges_in, 16)
                tail = EDGE_TAIL - first
                sp.dma_start(tile[rows:rows + 1, CH - 1, 0:tail], dst[first + EDGE_ROWS * P:E]
                             .rearrange("(p j) -> p j", p=1)).then_inc(edges_in, 16)
            sp.dma_start(wl_raw[:], w_l.rearrange("(k p) n -> p k n", p=P)).then_inc(weights_in, 16)
            sp.dma_start(wr_raw[:], w_r.rearrange("(k p) n -> p k n", p=P)).then_inc(weights_in, 16)
            sp.dma_start(bias_rows[:], bias.rearrange("(a n) -> a n", a=1).to_broadcast([P, D])).then_inc(bias_in, 16)

            def store_c(t, q, u):
                b = u % 2
                wait(sp, c_made, t + 1)
                sp.dma_start(corr[bass.ts(t, P), :], c_out[:, b]).then_inc(c_stored[b], 16)
            edge_steps(sp, store_c)

            sp.wait_ge(rows_moved, 1)

            def load_x(t, q, u):
                nt, rows = pair_shape(t)
                b, used = ring(q, u, 0, 4, 4)
                wait(sp, u_made, t - 3)
                if nt == 2:
                    sp.dma_start(X[:, b], x[bass.ts(t, 2 * P), :].rearrange("(a p) n -> p a n", p=P)
                                 ).then_inc(x_in[b], 16)
                else:
                    sp.dma_start(X[0:rows, b, 0], x[t * 2 * P:N, :]).then_inc(x_in[b], 16)

            def store_out(t, q, u):
                nt, rows = pair_shape(t)
                b = u % 2
                wait(sp, normed, t + 1)
                if nt == 2:
                    sp.dma_start(out[bass.ts(t, 2 * P), :].rearrange("(a p) n -> p a n", p=P), O[:, b]
                                 ).then_inc(stored[b], 16)
                else:
                    sp.dma_start(out[t * 2 * P:N, :], O[0:rows, b, 0]).then_inc(stored[b], 16)

            for t in range(3):
                load_x(t, 0, t)

            def move(t, q, u):
                if there(t + 3, NP):
                    load_x(t + 3, q + (u + 3) // 4, (u + 3) % 4)
                if there(t - 2, NP):
                    store_out(t - 2, q + (u - 2) // 4, (u - 2) % 4)
            pair_steps(sp, move)
            for t in (NP - 2, NP - 1):
                store_out(t, t // 4, t % 4)
            for b in range(2):
                sp.wait_ge(stored[b], 16 * (NP // 2))

        @block.gpsimd
        def _(pool):
            g = nc.gpsimd
            g.memset(e_dst[:, CH - 1], 0).then_inc(pads_zero, 1)
            g.memset(e_next[:, CH - 1], 0).then_inc(pads_zero, 1)
            g.iota(e_pos, [[P * P, CH], [1, P]], base=0, channel_multiplier=P).then_inc(pos_made, 1)
            g.iota(r_pos, [[P, ET]], base=0, channel_multiplier=1).then_inc(pos_made, 1)
            g.memset(eye3[:], 0.0).then_inc(eye_clear, 1)
            pool.wait_ge(eye_clear, 1)
            g.affine_select(out=eye3[:], in_=eye3[:], compare_op=ALU.not_equal, fill=1.0, base=P,
                            pattern=[[-1, 3 * P]], channel_multiplier=1).then_inc(consts, 1)
            g.memset(ones[:], 1.0).then_inc(consts, 1)
            g.memset(zeros[:], 0.0).then_inc(consts, 1)
            g.memset(minus_half[:], -0.5).then_inc(consts, 1)
            g.memset(dst_f[:, 0:1], -1.0).then_inc(consts, 1)
            pool.wait_ge(weights_in, 32)
            g.tensor_tensor(w_sum[:], wl_raw[:], wr_raw[:], ALU.add).then_inc(w_summed, 1)
            pool.wait_ge(w_rounded, 1)
            g.tensor_tensor(wl_lo[:], wl_raw[:], wl_hi[:].bitcast(f32), ALU.subtract).then_inc(w_split, 1)
            pool.wait_ge(w_rounded, 2)
            g.tensor_tensor(ws_lo[:], w_sum[:], ws_hi[:].bitcast(f32), ALU.subtract).then_inc(w_split, 1)
            pool.wait_ge(dst_ready, 1)
            g.affine_select(out=dst_c[:, ET - 1:ET], in_=dst_c[:, ET - 1:ET], compare_op=ALU.is_ge,
                            fill=float(N), base=R_LAST - 1, pattern=[[0, 1]], channel_multiplier=-1
                            ).then_inc(dst_padded, 1)

            def gather(out_, table, idx, rows, bound, s):
                g.indirect_dma_start(out=out_, out_offset=None, in_=table,
                                     in_offset=bass.IndirectOffsetOnAxis(ap=idx, axis=0),
                                     bounds_check=bound, oob_is_err=False).then_inc(s, 16)

            pool.wait_ge(dst_found, 1)

            def gather_xs(t, q, u):
                b, used = ring(q, u, 0, 2, 2)
                wait(pool, diff_made, t - 1)
                pool.wait_ge(src_in[b], 16 * (used + 1))
                pool.sem_inc(gate, 1)
                gather(xs[b][:], x, src_now[b][:, 0:1], P, N - 1, xs_in[b])

            def gather_edges(t, q, u):
                b, used = ring(q, u, 0, 2, 2)
                wait(pool, xs_in[b], 16 * used)
                wait(pool, xd_in[b], 16 * used)
                wait(pool, diff_made, t - 1)
                pool.sem_inc(gate, 1)
                g.tensor_copy(edge_now[b][:], edge_idx[:, bass.ds(t, 1)]).then_inc(now_copied, 1)
                g.tensor_copy(dst_now[b][:], dst_idx[:, bass.ds(t, 1)]).then_inc(now_copied, 1)
                pool.wait_ge(now_copied, 2 * t + 2)
                pool.sem_inc(gate, 1)
                gather(src_now[b][:], src_rows, edge_now[b][:, 0:1], P, E - 1, src_in[b])
                gather(xd[b][:], x, dst_now[b][:, 0:1], P, N - 1, xd_in[b])
                if there(t - 1, ET):
                    gather_xs(t - 1, q + (u - 1) // 2, (u - 1) % 2)
            edge_steps(pool, gather_edges)
            gather_xs(ET - 1, (ET - 1) // 2, (ET - 1) % 2)

            for b in range(2):
                pool.wait_ge(c_stored[b], 16 * (ET // 2))
            pool.wait_ge(idx_ready, 1)
            pool.wait_ge(bias_in, 16)
            wide_bias = bias_rows[:]

            def gather_cor(t, q, u):
                nt, rows = pair_shape(t)
                b, used = ring(q, u, 0, 4, 4)
                wait(pool, z_made, t - 3)
                if not fixed(t) or t > 3:
                    pool.sem_inc(gate, 1)
                g.tensor_copy(node_now[b][:, 0:nt], node_idx[:, bass.ds(2 * t, nt)]).then_inc(cor_reset, 1)
                for a in range(2):
                    g.tensor_scalar(cor[b][:, a], wide_bias, 1.0, 0.0, ALU.mult, ALU.add).then_inc(cor_reset, 1)
                pool.wait_ge(cor_reset, 3 * t + 3)
                pool.sem_inc(gate, 1)
                for a in range(nt):
                    gather(cor[b][0:rows, a], corr, node_now[b][0:rows, a:a + 1], rows, ET * P - 1, cor_in[b])

            def make_rstd(t, q, u):
                nt, rows = pair_shape(t)
                b = u % 2
                wait(pool, mv_made, 2 * t + 2)
                wait(pool, shift_made, t - 1)
                wait(pool, normed, t - 1)
                pool.sem_inc(gate, 1)
                g.tensor_scalar(var_eps[0:rows, b, 0:nt], mv[0:rows, b, 0:nt, 1], EPS, None, ALU.add
                                ).then_inc(eps_added, 1)
                pool.wait_ge(eps_added, t + 1)
                g.tensor_tensor(rstd[0:rows, b, 0:nt], var_eps[0:rows, b, 0:nt], minus_half[0:rows, 0:nt], ALU.pow
                                ).then_inc(rstd_made, 1)

            for t in range(2):
                gather_cor(t, 0, t)

            def serve(t, q, u):
                if there(t - 2, NP):
                    make_rstd(t - 2, q + (u - 2) // 4, (u - 2) % 4)
                if there(t + 2, NP):
                    gather_cor(t + 2, q + (u + 2) // 4, (u + 2) % 4)
            pair_steps(pool, serve)
            for t in (NP - 2, NP - 1):
                make_rstd(t, t // 4, t % 4)

        @block.tensor
        def _(pe):
            mm = nc.tensor.matmul
            pe.wait_ge(consts, 5)
            pe.wait_ge(rows_moved, 1)
            for a in range(2):
                bank = pT[0][:, a, :]
                for c in range(CH):
                    mm(bank[:, c * P:(c + 1) * P], rowed_f[:, a * CH + c, P:2 * P], eye, start=(c == 0), stop=False)
                for c in range(CH):
                    lo = 1 if c == 0 else 0
                    last = mm(bank[:, c * P - 1 + lo:(c + 1) * P - 1], rowed_f[:, a * CH + c, 0:P],
                              eye[:, lo:P], start=False, stop=(c == CH - 1))
            last.then_inc(merged, 1)
            pe.wait_ge(dst_found, 1)
            nc.tensor.transpose(pT[1][0:ET, 1, 0:P], dst_f[:, 1:1 + ET], eye)
            mm(pT[1][0:ET, 1, P:P + 1], dst_f[:, 0:ET], eye[:, P - 1:P], start=True, stop=True).then_inc(t_ready, 1)
            pe.wait_ge(upto_ready, 1)
            mm(pT[1][:, 0, 0:NTILES], eye3[:, P - 1:2 * P - 1], upto[:, 1:1 + NTILES], start=True, stop=False)
            mm(pT[1][:, 0, 0:NTILES], eye3[:, 2 * P - 1:3 * P - 1], upto[:, 0:NTILES], start=False, stop=True
               ).then_inc(before_ready, 1)
            pe.wait_ge(t_scanned, 1)
            mm(pH[0][0:1, 0, 0:ET], t_run[0:ET, P - 1:P], eye[0:ET, 0:ET], start=True, stop=True)
            mm(pH[0][0:1, 0, P:P + ET], t_whole[0:ET, P - 1:P], eye[0:ET, 0:ET], start=True, stop=True
               ).then_inc(ends_ready, 1)
            pe.wait_ge(carry_ready, 1)
            mm(pH[0][0:ET, 1, 0:1], row_ends[0:1, 2, 0:ET], ones[0:1, 0:1], start=True, stop=True
               ).then_inc(carry_col, 1)
            pe.wait_ge(t_deg, 1)
            nc.tensor.transpose(pH[1][:, 0, 0:ET], t_rdeg[0:ET, :], eye[0:ET, 0:ET]).then_inc(rdeg_ps, 1)

            def three(ps, hi, lo, w_hi, w_lo):
                terms = [(a, w, k) for a, w in ((hi, w_hi), (hi, w_lo), (lo, w_hi)) for k in range(K)]
                for n, (a, w, k) in enumerate(terms):
                    last = mm(ps, a[:, k], w[:, k], start=(n == 0), stop=(n == len(terms) - 1))
                return last

            def spread(t, q, u):
                b = u % 2
                wait(pe, wide_made, t + 1)
                wait(pe, row_kept, t - 1)
                nc.tensor.transpose(pT[b][:, 1, 0:P], dst_wide[b][:], eye).then_inc(row_made, 1)

            def combine(t, q, u):
                b = u % 2
                wait(pe, sames_made, 2 * t + 2)
                wait(pe, diff_made, t + 1)
                wait(pe, s_lo_made, t - 1)
                wait(pe, sums_made, t - 1)
                for k in range(K):
                    last = mm(pT[b][:, 0, k * P:(k + 1) * P], diff[b][:, k * P:(k + 1) * P], same[b][:],
                              start=True, stop=True)
                last.then_inc(summed, 1)

            for t in range(3):
                spread(t, 0, t)
            pe.wait_ge(rdeg_ready, 1)
            combine(0, 0, 0)
            pe.wait_ge(w_split, 2)

            def edge_tile(t, q, u):
                if there(t + 3, ET):
                    spread(t + 3, q + (u + 3) // 2, (u + 3) % 2)
                if there(t + 1, ET):
                    combine(t + 1, q + (u + 1) // 2, (u + 1) % 2)
                b = u % 2
                wait(pe, s_hi_made, t + 1)
                wait(pe, s_lo_made, t + 1)
                wait(pe, c_made, t - 1)
                three(pH[b][:, 0, :], s_hi[b], s_lo[b], wl_hi, wl_lo).then_inc(c_product, 1)
            edge_steps(pe, edge_tile)

            def transpose_x(t, q, u):
                nt, rows = pair_shape(t)
                b, used = ring(q, u, 0, 4, 4)
                pe.wait_ge(x_in[b], 16 * (used + 1))
                wait(pe, lo_made, t - 1)
                for a in range(nt):
                    for k in range(K):
                        last = nc.tensor.transpose(pT[u % 2][:, a, k * P:k * P + rows],
                                                   X[0:rows, b, a, k * P:(k + 1) * P], eye[0:rows, 0:rows])
                last.then_inc(transposed, 1)

            pe.wait_ge(c_made, ET)
            transpose_x(0, 0, 0)

            def node_pair(t, q, u):
                if there(t + 1, NP):
                    transpose_x(t + 1, q + (u + 1) // 4, (u + 1) % 4)
                nt, rows = pair_shape(t)
                b = u % 2
                wait(pe, hi_made, t + 1)
                wait(pe, lo_made, t + 1)
                wait(pe, z_made, t - 1)
                for a in range(nt):
                    last = three(pH[b][0:rows, a, :], x_hi[b][:, a, :, 0:rows], x_lo[b][:, a, :, 0:rows],
                                 ws_hi, ws_lo)
                last.then_inc(product, 1)
            pair_steps(pe, node_pair)

        @block.scalar
        def _(act):
            a_ = nc.scalar.activation
            act.preload_act_table_set("silu_and_others")
            act.wait_ge(weights_in, 32)
            a_(wl_hi[:], wl_raw[:], ACT.Copy).then_inc(w_rounded, 1)
            act.wait_ge(w_summed, 1)
            a_(ws_hi[:], w_sum[:], ACT.Copy).then_inc(w_rounded, 1)

            def widen(t, q, u):
                b = u % 2
                wait(act, row_made, t - 1)
                a_(dst_wide[b][:], dst_f[:, bass.ds(1 + t, 1)].to_broadcast([P, P]), ACT.Copy).then_inc(wide_made, 1)

            def keep_row(t, q, u):
                b = u % 2
                wait(act, row_made, t + 1)
                wait(act, sames_made, 2 * (t - 1))
                a_(dst_row[:, b, 1:1 + P], pT[b][:, 1, 0:P], ACT.Copy)
                if fixed(t) and t == 0:
                    a_(dst_row[:, b, 0:1], dst_f[:, 0:1], ACT.Copy).then_inc(row_kept, 1)
                else:
                    wait(act, row_kept, t)
                    a_(dst_row[:, b, 0:1], dst_row[:, 1 - b, P:1 + P], ACT.Copy).then_inc(row_kept, 1)

            def round_sums(t, q, u):
                b = u % 2
                wait(act, sums_made, t + 1)
                wait(act, c_product, t - 1)
                a_(s_hi[b][:], sums[:, b], ACT.Copy).then_inc(s_hi_made, 1)

            act.wait_ge(dst_found, 1)
            for t in range(4):
                widen(t, 0, t)
                if t < 3:
                    keep_row(t, 0, t)
            round_sums(0, 0, 0)

            def edge_tile(t, q, u):
                if there(t + 4, ET):
                    widen(t + 4, q + (u + 4) // 2, (u + 4) % 2)
                if there(t + 3, ET):
                    keep_row(t + 3, q + (u + 3) // 2, (u + 3) % 2)
                if there(t + 1, ET):
                    round_sums(t + 1, q + (u + 1) // 2, (u + 1) % 2)
            edge_steps(act, edge_tile)

            def round_x(t, q, u):
                nt, rows = pair_shape(t)
                b = u % 2
                wait(act, transposed, t + 1)
                wait(act, product, t - 1)
                a_(x_hi[b][:, 0:nt, :, 0:rows],
                   pT[b][:, 0:nt].rearrange("p a (k r) -> p a k r", k=K)[:, :, :, 0:rows], ACT.Copy).then_inc(hi_made, 1)

            def normalise(t, q, u):
                nt, rows = pair_shape(t)
                b, used = ring(q, u, 0, 4, 2)
                wait(act, shift_made, t + 1)
                wait(act, stored[b], 16 * used)
                for a in range(nt):
                    last = a_(O[0:rows, b, a], Z[0:rows, b, a], ACT.Identity, scale=rstd[0:rows, b, a:a + 1],
                              bias=shift[0:rows, b, a:a + 1])
                last.then_inc(normed, 1)

            def silu(t, q, u):
                nt, rows = pair_shape(t)
                b = u % 2
                wait(act, z_made, t + 1)
                a_(Z[0:rows, b, 0:nt], Z[0:rows, b, 0:nt], ACT.Silu).then_inc(silu_made, 1)

            round_x(0, 0, 0)

            def node_pair(t, q, u):
                if there(t + 1, NP):
                    round_x(t + 1, q + (u + 1) // 4, (u + 1) % 4)
                if there(t - 2, NP):
                    normalise(t - 2, q + (u - 2) // 4, (u - 2) % 4)
                if there(t - 1, NP):
                    silu(t - 1, q + (u - 1) // 4, (u - 1) % 4)
            pair_steps(act, node_pair)
            silu(NP - 1, (NP - 1) // 4, (NP - 1) % 4)
            for t in (NP - 2, NP - 1):
                normalise(t, t // 4, t % 4)

        @block.vector
        def _(dve):
            v = nc.vector
            done = [0]

            def then(ins):
                done[0] += 1
                ins.then_inc(dve_step, 1)
                dve.wait_ge(dve_step, done[0])

            v.memset(rowed[0], 0)
            then(v.memset(rowed[1], 0))
            dve.wait_ge(edges_in, 96)
            dve.wait_ge(pos_made, 2)
            v.tensor_tensor(e_rank, e_pos, e_dst, ALU.subtract)
            v.tensor_tensor(e_loop, e_dst, e_next, ALU.not_equal)
            then(v.tensor_tensor(e_other, e_dst, e_next, ALU.is_equal))
            v.tensor_tensor(rowed[0][:, 0:CH, P:], e_dst, e_other, ALU.mult)
            then(v.tensor_tensor(rowed[0][:, CH:, P:], e_rank, e_loop, ALU.mult))

            def move_left(out_, in_, mask, k, step, lo, hi, n):
                then(v.tensor_scalar(mask[:, :, lo:hi], in_[:, :, lo:hi], 31 - k, 31,
                                     ALU.logical_shift_left, ALU.arith_shift_right))
                then(v.scalar_tensor_tensor(out_[:, :, lo:hi], mask[:, :, lo:hi], -1, in_[:, :, lo:hi],
                                            ALU.bitwise_xor, ALU.bitwise_and))
                to = max(lo - step, 0)
                then(v.copy_predicated(out_[:, :, to:hi - step], mask[:, :, to + step:hi], in_[:, :, to + step:hi]))

            for k in range(ROW_BITS):
                move_left(rowed[(k + 1) % 2], rowed[k % 2], row_mask, k, 1 << k, P - (1 << k) + 1, 2 * P, None)
            then(v.tensor_copy(rowed_f[:], rowed[ROW_BITS % 2]))
            dve.sem_inc(rows_moved, 1)
            dve.wait_ge(merged, 1)
            then(v.tensor_copy(col[0], pT[0][:]))
            for k in range(ROW_BITS, BITS):
                n = k - ROW_BITS
                move_left(col[(n + 1) % 2], col[n % 2], col_mask, k, 1 << n, 0, COLS, None)
            found = col[(BITS - ROW_BITS) % 2]
            v.tensor_copy(dst_c, found[:, 0, 0:ET]).then_inc(dst_ready, 1)
            v.memset(upto[:, 0:1], 0.0)
            v.tensor_copy(upto[:, 1:1 + NTILES], found[:, 1, 0:NTILES]).then_inc(upto_ready, 1)
            dve.wait_ge(dst_padded, 1)
            then(v.tensor_tensor(edge_idx[:], dst_c, r_pos, ALU.add))
            v.tensor_scalar(edge_idx[:], edge_idx[:], E - 1.0, None, ALU.min)
            v.tensor_scalar(dst_idx[:], dst_c, N - 1.0, None, ALU.min)
            then(v.tensor_copy(dst_f[:, 1:1 + ET], dst_c))
            dve.sem_inc(dst_found, 1)
            dve.wait_ge(consts, 5)
            dve.wait_ge(t_ready, 1)
            v.tensor_copy(t_dst[0:ET, 1:1 + P], pT[1][0:ET, 1, 0:P])
            then(v.tensor_copy(t_dst[0:ET, 0:1], pT[1][0:ET, 1, P:P + 1]))
            then(v.tensor_tensor(t_same[0:ET], t_dst[0:ET, 1:1 + P], t_dst[0:ET, 0:P], ALU.is_equal))
            v.tensor_tensor_scan(t_run[0:ET], t_same[0:ET], ones[0:ET, :], 0.0, ALU.mult, ALU.add)
            v.tensor_tensor_scan(t_whole[0:ET], t_same[0:ET], zeros[0:ET, :], 1.0, ALU.mult, ALU.add
                                 ).then_inc(t_scanned, 1)
            dve.wait_ge(before_ready, 1)
            then(v.tensor_tensor(none, upto[:, 1:1 + NTILES], pT[1][:, 0, 0:NTILES], ALU.subtract))
            then(v.tensor_scalar(none, none, 0.0, float(SKIP), ALU.is_equal, ALU.mult))
            v.memset(node_idx[:, NTILES:NTILES + 1], SKIP)
            v.scalar_tensor_tensor(node_idx[:, 0:NTILES], upto[:, 1:1 + NTILES], -1.0, none, ALU.add, ALU.add
                                   ).then_inc(idx_ready, 1)
            dve.wait_ge(ends_ready, 1)
            v.memset(row_ends[0:1, 2, 0:1], 0.0)
            then(v.tensor_copy(row_ends[0:1, 0:2, 0:ET],
                               pH[0][0:1, 0, 0:2 * P].rearrange("p (a c) -> p a c", a=2)[:, :, 0:ET]))
            v.tensor_tensor_scan(row_ends[0:1, 2, 1:ET], row_ends[0:1, 1, 0:ET - 1], row_ends[0:1, 0, 0:ET - 1], 0.0,
                                 ALU.mult, ALU.add).then_inc(carry_ready, 1)
            dve.wait_ge(carry_col, 1)
            then(v.scalar_tensor_tensor(t_count[0:ET], t_whole[0:ET], pH[0][0:ET, 1, 0:1], t_run[0:ET],
                                        ALU.mult, ALU.add))
            then(v.tensor_scalar(t_count[0:ET], t_count[0:ET], 1.0, None, ALU.add))
            v.reciprocal(t_rdeg[0:ET], t_count[0:ET]).then_inc(t_deg, 1)
            dve.wait_ge(rdeg_ps, 1)
            then(v.tensor_copy(rdeg[:], pH[1][:, 0, 0:ET]))
            dve.sem_inc(rdeg_ready, 1)
            dve.wait_ge(bias_in, 16)

            def compare(t, q, u):
                b, used = ring(q, u, 0, 2, 2)
                wait(dve, row_kept, t + 1)
                wait(dve, summed, t - 1)
                v.tensor_scalar(same[b][:], dst_row[:, b, 1:1 + P], dst_f[:, bass.ds(1 + t, 1)], None, ALU.is_equal
                                ).then_inc(sames_made, 1)
                v.tensor_scalar(goes_on[:, b], dst_row[:, b, 1:1 + P], dst_row[:, b, 0:1], None, ALU.is_equal
                                ).then_inc(sames_made, 1)
                dve.wait_ge(xs_in[b], 16 * (used + 1))
                dve.wait_ge(xd_in[b], 16 * (used + 1))
                v.tensor_tensor(diff[b][:], xs[b][:], xd[b][:], ALU.subtract).then_inc(diff_made, 1)

            def carry(t, q, u):
                b = u % 2
                wait(dve, summed, t + 1)
                wait(dve, sums_made, t)
                wait(dve, s_lo_made, t)
                wait(dve, s_hi_made, t - 1)
                for k in range(K):
                    last = v.scalar_tensor_tensor(
                        sums[:, b, k], goes_on[:, b], zeros[:, 0:1] if fixed(t) and t == 0 else sums[:, 1 - b, k, P - 1:P],
                        pT[b][:, 0, k * P:(k + 1) * P], ALU.mult, ALU.add)
                last.then_inc(sums_made, 1)
                wait(dve, s_hi_made, t + 1)
                wait(dve, c_product, t - 1)
                v.tensor_tensor(s_lo[b][:], sums[:, b], s_hi[b][:].bitcast(f32), ALU.subtract).then_inc(s_lo_made, 1)

            def finish(t, q, u):
                b, used = ring(q, u, 0, 2, 2)
                wait(dve, c_product, t + 1)
                wait(dve, c_stored[b], 16 * used)
                v.scalar_tensor_tensor(c_out[:, b], pH[b][:, 0, :], rdeg[:, bass.ds(t, 1)], bias_rows[:],
                                       ALU.mult, ALU.add).then_inc(c_made, 1)

            compare(0, 0, 0)
            compare(1, 0, 1)
            carry(0, 0, 0)

            def edge_tile(t, q, u):
                if there(t - 1, ET):
                    finish(t - 1, q + (u - 1) // 2, (u - 1) % 2)
                if there(t + 1, ET):
                    carry(t + 1, q + (u + 1) // 2, (u + 1) % 2)
                if there(t + 2, ET):
                    compare(t + 2, q + (u + 2) // 2, (u + 2) % 2)
            edge_steps(dve, edge_tile)
            finish(ET - 1, (ET - 1) // 2, (ET - 1) % 2)

            def split_x(t, q, u):
                nt, rows = pair_shape(t)
                b = u % 2
                wait(dve, hi_made, t + 1)
                v.tensor_tensor(x_lo[b][:, 0:nt, :, 0:rows],
                                pT[b][:, 0:nt].rearrange("p a (k r) -> p a k r", k=K)[:, :, :, 0:rows],
                                x_hi[b][:, 0:nt, :, 0:rows].bitcast(f32), ALU.subtract).then_inc(lo_made, 1)

            def add_cor(t, q, u):
                nt, rows = pair_shape(t)
                b, used = ring(q, u, 0, 4, 4)
                wait(dve, product, t + 1)
                if nt == 2:
                    dve.wait_ge(cor_in[b], 32 * (used + 1))
                else:
                    dve.wait_ge(cor_in[b], 32 * used + 16)
                wait(dve, normed, t - 1)
                v.tensor_tensor(Z[0:rows, u % 2, 0:nt], pH[u % 2][0:rows, 0:nt], cor[b][0:rows, 0:nt], ALU.add
                                ).then_inc(z_made, 1)

            def residual(t, q, u):
                nt, rows = pair_shape(t)
                b = u % 4
                wait(dve, silu_made, t + 1)
                v.tensor_tensor(Z[0:rows, u % 2, 0:nt], Z[0:rows, u % 2, 0:nt], X[0:rows, b, 0:nt], ALU.add
                                ).then_inc(u_made, 1)
                wait(dve, u_made, t + 1)
                wait(dve, rstd_made, t - 1)
                for a in range(nt):
                    v.bn_stats(stats[0:rows, u % 2, a], Z[0:rows, u % 2, a]).then_inc(stats_made, 1)
                wait(dve, stats_made, 2 * t + nt)
                dve.sem_inc(dve_gate, 1)
                for a in range(nt):
                    v.bn_aggr(mv[0:rows, u % 2, a], stats[0:rows, u % 2, a]).then_inc(mv_made, 3 - nt)

            def make_shift(t, q, u):
                nt, rows = pair_shape(t)
                b = u % 2
                wait(dve, rstd_made, t + 1)
                wait(dve, normed, t - 1)
                v.scalar_tensor_tensor(shift[0:rows, b, 0:nt], mv[0:rows, b, 0:nt, 0], -1.0, rstd[0:rows, b, 0:nt],
                                       ALU.mult, ALU.mult).then_inc(shift_made, 1)

            split_x(0, 0, 0)

            def node_pair(t, q, u):
                if there(t - 2, NP):
                    make_shift(t - 2, q + (u - 2) // 4, (u - 2) % 4)
                if there(t - 1, NP):
                    add_cor(t - 1, q + (u - 1) // 4, (u - 1) % 4)
                if there(t + 1, NP):
                    split_x(t + 1, q + (u + 1) // 4, (u + 1) % 4)
                if there(t - 1, NP):
                    residual(t - 1, q + (u - 1) // 4, (u - 1) % 4)
            pair_steps(dve, node_pair)
            t = NP - 1
            add_cor(t, t // 4, t % 4)
            make_shift(t - 1, (t - 1) // 4, (t - 1) % 4)
            residual(t, t // 4, t % 4)
            make_shift(t, t // 4, t % 4)


_INS = ["x", "src", "dst", "L0_gnn_W_l", "L0_gnn_W_r", "L0_gnn_b"]


def kernel(**inputs):
    import numpy as _np
    import concourse.bacc as _bacc
    from concourse import mybir as _mybir
    from concourse.bass_utils import run_bass_kernel_spmd as _run

    nc = _bacc.Bacc("TRN2", target_bir_lowering=False, num_devices=1)
    arrays, args = {}, []
    for name in _INS:
        a = _np.ascontiguousarray(inputs[name])
        arrays[f"in_{name}"] = a
        args.append(nc.dram_tensor(f"in_{name}", a.shape, _mybir.dt.from_np(a.dtype), kind="ExternalInput").ap())
    shape = tuple(inputs["x"].shape)
    args.append(nc.dram_tensor("out_0", shape, _mybir.dt.float32, kind="ExternalOutput").ap())
    gnn_layer(nc, *args)
    r = _run(nc, [arrays], core_ids=[0])
    return r.results[0]["out_0"]
```

```python
from contextlib import ExitStack

import concourse.bass as bass
from concourse import mybir


def gnn_layer(nc, x, src, dst, w_l, w_r, bias, out):
    f32, f32r, i32 = mybir.dt.float32, mybir.dt.float32r, mybir.dt.int32
    ALU = mybir.AluOpType
    ACT = mybir.ActivationFunctionType
    P = nc.NUM_PARTITIONS

    N, D = x.shape
    E = src.shape[0]
    R = E - N
    K = D // P
    EPS = 1e-5

    EDGE_ROWS, EDGE_TAIL = E // P, E % P
    CH = -(-(EDGE_ROWS + 1) // P)
    FULL = (CH - 1) * P
    COLS = CH * P
    ROW_BITS = P.bit_length() - 1
    BITS = (N - 1).bit_length()
    ET = -(-R // P)
    R_LAST = R - (ET - 1) * P
    NTILES = -(-N // P)
    N_LAST = N - (NTILES - 1) * P
    EARLY = 44
    BASE = EARLY * P
    NP = -(-(NTILES - EARLY) // 2)
    SKIP = 1 << 20
    assert (NTILES - EARLY) % 2 == 1 and ET % 2 == 0 and NP % 2 == 0 and COLS <= 512
    assert EARLY - 1 == NP // 4
    assert BITS - ROW_BITS <= COLS.bit_length()

    corr = nc.dram_tensor("correction_rows", (ET * P, D), f32, kind="Internal").ap()
    early_product = nc.dram_tensor("early_product", (BASE, D), f32, kind="Internal").ap()
    src_rows = src.rearrange("(e a) -> e a", a=1)

    ctx = ExitStack()
    with ctx:
        def sb(name, shape, dt):
            return ctx.enter_context(nc.sbuf_tensor(name, shape, dt))

        def sem(name):
            return ctx.enter_context(nc.semaphore(name))

        eye3 = sb("eye3", [P, 3 * P], f32)
        eye = eye3[:, P:2 * P]
        ones = sb("ones", [P, P], f32)
        zeros = sb("zeros", [P, P], f32)
        minus_half = sb("minus_half", [P, 2], f32)
        bias_rows = sb("bias_rows", [P, D], f32)
        wl_raw = sb("wl_raw", [P, K, D], f32)
        wr_raw = sb("wr_raw", [P, K, D], f32)
        w_sum = sb("w_sum", [P, K, D], f32)
        ws_hi, ws_lo = sb("ws_hi", [P, K, D], f32r), sb("ws_lo", [P, K, D], f32r)
        wl_hi, wl_lo = sb("wl_hi", [P, K, D], f32r), sb("wl_lo", [P, K, D], f32r)
        X = sb("X", [P, 4, 2, D], f32)
        x_hi = [sb(f"x_hi{b}", [P, 2, K, P], f32r) for b in range(2)]
        x_lo = [sb(f"x_lo{b}", [P, 2, K, P], f32r) for b in range(2)]
        cor = [sb(f"cor{b}", [P, 2, D], f32) for b in range(4)]
        Z = sb("Z", [P, 4, 2, D], f32)
        O = sb("O", [P, 2, 2, D], f32)
        stats = sb("stats", [P, 2, 2, nc.vector.BN_STATS_DIM], f32)
        mv = sb("mv", [P, 2, 2, 2], f32)
        var_eps = sb("var_eps", [P, 2, 2], f32)
        rstd = sb("rstd", [P, 2, 2], f32)
        shift = sb("shift", [P, 2, 2], f32)
        node_idx = sb("node_idx", [P, NTILES + 1], i32)
        node_now = [sb(f"node_now{b}", [P, 2], i32) for b in range(4)]
        l_x, l_h, l_cor, l_z, l_u, l_o = (sb(f"light_{n}", [P, D], f32) for n in ("x", "h", "cor", "z", "u", "o"))
        l_stats, l_mv = sb("l_stats", [P, nc.vector.BN_STATS_DIM], f32), sb("l_mv", [P, 2], f32)
        l_var_eps, l_rstd, l_shift = sb("l_var_eps", [P, 1], f32), sb("l_rstd", [P, 1], f32), sb("l_shift", [P, 1], f32)
        l_now = sb("l_now", [P, 1], i32)
        e_x, e_t, e_out = (l_x, l_h), (l_cor, l_z), (l_u, l_o)
        edge_idx = sb("edge_idx", [P, ET, 2], i32)
        dst_f = sb("dst_f", [P, 1 + ET], f32)
        rdeg = sb("rdeg", [P, ET], f32)
        edge_now = [sb(f"edge_now{b}", [P, 2], i32) for b in range(4)]
        src_now = [sb(f"src_now{b}", [P, 1], i32) for b in range(4)]
        xs = [sb(f"xs{b}", [P, D], f32) for b in range(4)]
        xd = [sb(f"xd{b}", [P, D], f32) for b in range(4)]
        diff = [sb(f"diff{b}", [P, D], f32) for b in range(2)]
        dst_wide = [sb(f"dst_wide{b}", [P, P], f32) for b in range(2)]
        dst_row = sb("dst_row", [P, 2, 1 + P], f32)
        same = [sb(f"same{b}", [P, P], f32) for b in range(2)]
        goes_on = sb("goes_on", [P, 2, P], f32)
        sums = sb("sums", [P, 2, K, P], f32)
        s_hi = [sb(f"s_hi{b}", [P, K, P], f32r) for b in range(2)]
        s_lo = [sb(f"s_lo{b}", [P, K, P], f32r) for b in range(2)]
        c_out = sb("c_out", [P, 2, D], f32)
        Xi = X[:].bitcast(i32)
        rowed = [Xi[:, 2 * b:2 * b + 2].rearrange("p a t (c j) -> p (a t c) j", j=2 * P) for b in range(2)]
        assert 2 * CH * 2 * P <= 2 * 2 * D
        row_mask = sb("row_mask", [P, 2 * CH, 2 * P], i32)
        rowed_f = sb("rowed_f", [P, 2 * CH, 2 * P], f32)
        col = [cor[b][:].bitcast(i32) for b in range(2)]
        col_mask = cor[2][:].bitcast(i32)
        e_dst = cor[3][:, 0].bitcast(i32).rearrange("p (c j) -> p c j", j=P)
        e_next = cor[3][:, 1].bitcast(i32).rearrange("p (c j) -> p c j", j=P)
        e_pos = Z[:, 0, 0].bitcast(i32).rearrange("p (c j) -> p c j", j=P)
        e_other = Z[:, 0, 1].bitcast(i32).rearrange("p (c j) -> p c j", j=P)
        e_loop = Z[:, 1, 0].bitcast(i32).rearrange("p (c j) -> p c j", j=P)
        e_rank = Z[:, 1, 1].bitcast(i32).rearrange("p (c j) -> p c j", j=P)
        upto = O[:, 0, 0, 0:1 + NTILES]
        none = O[:, 0, 1, 0:NTILES]
        r_pos = O[:, 1, 0, 0:ET].bitcast(i32)
        dst_c = O[:, 1, 0, P:P + ET].bitcast(i32)
        t_dst = O[:, 1, 1, 0:1 + P]
        t_same = O[:, 1, 1, P + 16:P + 16 + P]
        t_run = sums[:, 0, 0]
        t_whole = sums[:, 0, 1]
        t_count = sums[:, 0, 2]
        t_rdeg = sums[:, 0, 3]
        row_ends = sb("row_ends", [1, 3, P], f32)

        pT = [ctx.enter_context(nc.psum_tensor(f"pT{b}", [P, 2, D], f32)) for b in range(2)]
        pH = [ctx.enter_context(nc.psum_tensor(f"pH{b}", [P, 2, D], f32)) for b in range(2)]

        before_ps = pH[1][:, 0, 0:NTILES]
        t_dst_ps = pH[1][0:ET, 1, 0:P]
        t_before_ps = pH[1][0:ET, 1, P:P + 1]
        carry_ps = pH[1][0:ET, 1, P + 4:P + 5]
        ends_ps = pH[1][0:1, 1, P + 8:P + 8 + 2 * ET]
        rdeg_in_ps = pH[1][:, 1, 3 * P:3 * P + ET]

        pads_zero, edges_in, bias_in, weights_in = sem("pads_zero"), sem("edges_in"), sem("bias_in"), sem("weights_in")
        eye_clear, consts, pos_made = sem("eye_clear"), sem("consts"), sem("pos_made")
        w_summed, w_rounded, w_split = sem("w_summed"), sem("w_rounded"), sem("w_split")
        dve_step, rows_moved, merged = sem("dve_step"), sem("rows_moved"), sem("merged")
        dst_padded, dst_ready, dst_found = sem("dst_padded"), sem("dst_ready"), sem("dst_found")
        upto_ready, before_ready = sem("upto_ready"), sem("before_ready")
        t_ready, t_scanned, ends_ready, ends_copied = sem("t_ready"), sem("t_scanned"), sem("ends_ready"), sem("ends_copied")
        carry_ready, carry_col, t_deg, rdeg_ps, rdeg_ready = (sem("carry_ready"), sem("carry_col"), sem("t_deg"),
                                                             sem("rdeg_ps"), sem("rdeg_ready"))
        idx_ready = sem("idx_ready")
        gate, dve_gate = sem("gate"), sem("dve_gate")
        now_copied = sem("now_copied")
        src_in = [sem(f"src_in{b}") for b in range(4)]
        xs_in = [sem(f"xs_in{b}") for b in range(4)]
        xd_in = [sem(f"xd_in{b}") for b in range(4)]
        wide_made, row_made, row_kept, sames_made, diff_made = (sem("wide_made"), sem("row_made"), sem("row_kept"),
                                                               sem("sames_made"), sem("diff_made"))
        summed, sums_made, s_hi_made, s_lo_made, c_product, c_made = (sem("summed"), sem("sums_made"),
                                                                     sem("s_hi_made"), sem("s_lo_made"),
                                                                     sem("c_product"), sem("c_made"))
        c_stored = [sem(f"c_stored{b}") for b in range(2)]
        x_in = [sem(f"x_in{b}") for b in range(4)]
        cor_in = [sem(f"cor_in{b}") for b in range(4)]
        transposed, hi_made, lo_made, product, z_made, silu_made = (sem("transposed"), sem("hi_made"), sem("lo_made"),
                                                                   sem("product"), sem("z_made"), sem("silu_made"))
        u_made, stats_made, mv_made, eps_added, rstd_made, shift_made, normed = (
            sem("u_made"), sem("stats_made"), sem("mv_made"), sem("eps_added"), sem("rstd_made"),
            sem("shift_made"), sem("normed"))
        cor_reset, node_ready = sem("cor_reset"), sem("node_ready")
        stored = [sem(f"stored{b}") for b in range(2)]

        early_x_in = [sem(f"early_x_in{b}") for b in range(2)]
        early_stored = [sem(f"early_stored{b}") for b in range(2)]
        early_transposed, early_hi, early_copied, early_lo, early_done, early_kept = (
            sem("early_transposed"), sem("early_hi"), sem("early_copied"), sem("early_lo"),
            sem("early_done"), sem("early_kept"))
        light_in, light_now, light_reset, light_cor_in, light_z, light_silu, light_u = (
            sem("light_in"), sem("light_now"), sem("light_reset"), sem("light_cor_in"), sem("light_z"),
            sem("light_silu"), sem("light_u_made"))
        light_stats, light_mv, light_eps, light_rstd, light_shift, light_normed, light_stored = (
            sem("light_stats"), sem("light_mv"), sem("light_eps"), sem("light_rstd_made"),
            sem("light_shift"), sem("light_normed"), sem("light_stored"))

        block = ctx.enter_context(nc.Block())

        def fixed(v):
            return isinstance(v, int)

        def wait(eng, s, v):
            if not fixed(v) or v > 0:
                eng.wait_ge(s, v)

        def steps(eng, n, step):
            rounds = n // 4
            peeled(0, 8, step)
            looped(eng, 2, rounds - 1, step)
            peeled(4 * (rounds - 1), n, step)

        def peeled(first, end, step):
            for t in range(first, end):
                step(t, t // 4, t % 4)

        def looped(eng, first, end, step):
            with eng.Fori(first, end) as q:
                for u in range(4):
                    step(4 * q + u, q, u)

        def light_tail(light):
            for k in range(NP, 4 * EARLY + 8):
                light(k // 4, k % 4)

        def light_at(l, step):
            if not fixed(l) or 0 <= l < EARLY:
                step(l)

        def shifted(t, q, u, by, n, step):
            if not fixed(t) or 0 <= t + by < n:
                step(t + by, q + (u + by) // 4, (u + by) % 4)

        def single(t, step):
            step(t, t // 4, t % 4)

        def ring(q, u, n):
            return u % n, q * (4 // n) + u // n

        def pair_shape(j):
            return (1, N_LAST) if fixed(j) and j == NP - 1 else (2, P)

        @block.sync
        def _(sp):
            sp.wait_ge(pads_zero, 2)
            for tile, first in ((e_dst, 0), (e_next, 1)):
                sp.dma_start(tile[:, 0:CH - 1], dst[first:first + FULL * P].rearrange("(c p j) -> p c j", p=P, j=P)
                             ).then_inc(edges_in, 16)
                rows = EDGE_ROWS - FULL
                sp.dma_start(tile[0:rows, CH - 1], dst[first + FULL * P:first + EDGE_ROWS * P]
                             .rearrange("(p j) -> p j", j=P)).then_inc(edges_in, 16)
                tail = EDGE_TAIL - first
                sp.dma_start(tile[rows:rows + 1, CH - 1, 0:tail], dst[first + EDGE_ROWS * P:E]
                             .rearrange("(p j) -> p j", p=1)).then_inc(edges_in, 16)
            sp.dma_start(wl_raw[:], w_l.rearrange("(k p) n -> p k n", p=P)).then_inc(weights_in, 16)
            sp.dma_start(wr_raw[:], w_r.rearrange("(k p) n -> p k n", p=P)).then_inc(weights_in, 16)
            sp.dma_start(bias_rows[:], bias.rearrange("(a n) -> a n", a=1).to_broadcast([P, D])).then_inc(bias_in, 16)

            def load_early(t, q, u):
                b = u % 2
                wait(sp, early_transposed, t - 1)
                sp.dma_start(e_x[b][:], x[bass.ts(t, P), :]).then_inc(early_x_in[b], 16)

            def store_early(t, q, u):
                b = u % 2
                wait(sp, early_kept, t + 1)
                sp.dma_start(early_product[bass.ts(t, P), :], e_out[b][:]).then_inc(early_stored[b], 16)

            def move_early(t, q, u):
                shifted(t, q, u, 2, EARLY, load_early)
                shifted(t, q, u, -1, EARLY, store_early)
            single(0, load_early)
            single(1, load_early)
            steps(sp, EARLY, move_early)
            single(EARLY - 1, store_early)

            def store_c(t, q, u):
                b = u % 2
                wait(sp, c_made, t + 1)
                sp.dma_start(corr[bass.ts(t, P), :], c_out[:, b]).then_inc(c_stored[b], 16)
            steps(sp, ET, store_c)

            sp.wait_ge(rows_moved, 1)

            def load_x(t, q, u):
                nt, rows = pair_shape(t)
                b, used = ring(q, u, 4)
                wait(sp, u_made, t - 3)
                if nt == 2:
                    sp.dma_start(X[:, b], x[bass.ds(BASE + t * 2 * P, 2 * P), :].rearrange("(a p) n -> p a n", p=P)
                                 ).then_inc(x_in[b], 16)
                else:
                    sp.dma_start(X[0:rows, b, 0], x[BASE + t * 2 * P:N, :]).then_inc(x_in[b], 16)

            def store_out(t, q, u):
                nt, rows = pair_shape(t)
                b = u % 2
                wait(sp, normed, t + 1)
                if nt == 2:
                    sp.dma_start(out[bass.ds(BASE + t * 2 * P, 2 * P), :].rearrange("(a p) n -> p a n", p=P), O[:, b]
                                 ).then_inc(stored[b], 16)
                else:
                    sp.dma_start(out[BASE + t * 2 * P:N, :], O[0:rows, b, 0]).then_inc(stored[b], 16)

            for t in range(3):
                single(t, load_x)

            def load_light(l):
                wait(sp, light_u, l)
                sp.dma_start(l_x[:], x[bass.ts(l, P), :]).then_inc(light_in, 16)
                sp.dma_start(l_h[:], early_product[bass.ts(l, P), :]).then_inc(light_in, 16)

            def store_light(l):
                wait(sp, light_normed, l + 1)
                sp.dma_start(out[bass.ts(l, P), :], l_o[:]).then_inc(light_stored, 16)

            def light(q, u):
                if u == 2:
                    light_at(q - 1, store_light)
                if u == 3:
                    light_at(q + 1, load_light)
            for b in range(2):
                sp.wait_ge(early_stored[b], 16 * (EARLY // 2))
            load_light(0)

            def move(t, q, u):
                shifted(t, q, u, 3, NP, load_x)
                shifted(t, q, u, -3, NP, store_out)
                light(q, u)
            steps(sp, NP, move)
            for t in range(NP - 3, NP):
                single(t, store_out)
            light_tail(light)
            sp.wait_ge(light_stored, 16 * EARLY)
            for b in range(2):
                sp.wait_ge(stored[b], 16 * (NP // 2))

        @block.gpsimd
        def _(pool):
            g = nc.gpsimd
            g.memset(e_dst[:, CH - 1], 0).then_inc(pads_zero, 1)
            g.memset(e_next[:, CH - 1], 0).then_inc(pads_zero, 1)
            g.iota(e_pos, [[P * P, CH], [1, P]], base=0, channel_multiplier=P).then_inc(pos_made, 1)
            g.iota(r_pos, [[P, ET]], base=0, channel_multiplier=1).then_inc(pos_made, 1)
            g.memset(eye3[:], 0.0).then_inc(eye_clear, 1)
            pool.wait_ge(eye_clear, 1)
            g.affine_select(out=eye3[:], in_=eye3[:], compare_op=ALU.not_equal, fill=1.0, base=P,
                            pattern=[[-1, 3 * P]], channel_multiplier=1).then_inc(consts, 1)
            g.memset(ones[:], 1.0).then_inc(consts, 1)
            g.memset(zeros[:], 0.0).then_inc(consts, 1)
            g.memset(minus_half[:], -0.5).then_inc(consts, 1)
            g.memset(dst_f[:, 0:1], -1.0).then_inc(consts, 1)
            pool.wait_ge(weights_in, 32)
            g.tensor_tensor(w_sum[:], wl_raw[:], wr_raw[:], ALU.add).then_inc(w_summed, 1)
            pool.wait_ge(w_rounded, 1)
            g.tensor_tensor(ws_lo[:], w_sum[:], ws_hi[:].bitcast(f32), ALU.subtract).then_inc(w_split, 1)

            def split_early(t, q, u):
                b = u % 2
                wait(pool, early_copied, t + 1)
                wait(pool, early_done, t - 1)
                g.tensor_tensor(x_lo[b][:, 0], e_t[b][:].rearrange("p (k r) -> p k r", k=K),
                                x_hi[b][:, 0].bitcast(f32), ALU.subtract).then_inc(early_lo, 1)
            peeled(0, 4, split_early)
            pool.wait_ge(w_rounded, 2)
            for k in range(K):
                g.tensor_tensor(wl_lo[:, k], wl_raw[:, k], wl_hi[:, k].bitcast(f32), ALU.subtract
                                ).then_inc(w_split, 1)
                peeled(4 + k, 5 + k, split_early)
            looped(pool, 2, 5, split_early)
            pool.wait_ge(dst_ready, 1)
            g.affine_select(out=dst_c[:, ET - 1:ET], in_=dst_c[:, ET - 1:ET], compare_op=ALU.is_ge,
                            fill=float(N), base=R_LAST - 1, pattern=[[0, 1]], channel_multiplier=-1
                            ).then_inc(dst_padded, 1)
            looped(pool, 5, EARLY // 4, split_early)

            def gather(out_, table, idx, rows, bound, s):
                g.indirect_dma_start(out=out_, out_offset=None, in_=table,
                                     in_offset=bass.IndirectOffsetOnAxis(ap=idx, axis=0),
                                     bounds_check=bound, oob_is_err=False).then_inc(s, 16)

            pool.wait_ge(dst_found, 1)

            def gather_xs(t, q, u):
                b, used = ring(q, u, 4)
                pool.wait_ge(src_in[b], 16 * (used + 1))
                pool.sem_inc(gate, 1)
                gather(xs[b][:], x, src_now[b][:, 0:1], P, N - 1, xs_in[b])

            def gather_edges(t, q, u):
                b, used = ring(q, u, 4)
                if not fixed(t) or t > 3:
                    wait(pool, diff_made, t - 3)
                    pool.sem_inc(gate, 1)
                g.tensor_copy(edge_now[b][:], edge_idx[:, bass.ds(t, 1)].rearrange("p t a -> p (t a)")
                              ).then_inc(now_copied, 1)
                pool.wait_ge(now_copied, t + 1)
                pool.sem_inc(gate, 1)
                gather(src_now[b][:], src_rows, edge_now[b][:, 0:1], P, E - 1, src_in[b])
                gather(xd[b][:], x, edge_now[b][:, 1:2], P, N - 1, xd_in[b])
                shifted(t, q, u, -1, ET, gather_xs)
            steps(pool, ET, gather_edges)
            single(ET - 1, gather_xs)

            for b in range(2):
                pool.wait_ge(c_stored[b], 16 * (ET // 2))
            pool.wait_ge(idx_ready, 1)

            def gather_cor(t, q, u):
                nt, rows = pair_shape(t)
                b, used = ring(q, u, 4)
                wait(pool, cor_reset, t + 1)
                pool.sem_inc(gate, 1)
                g.tensor_copy(node_now[b][:, 0:nt], node_idx[:, bass.ds(EARLY + 2 * t, nt)]).then_inc(node_ready, 1)
                pool.wait_ge(node_ready, t + 1)
                pool.sem_inc(gate, 1)
                for a in range(nt):
                    gather(cor[b][0:rows, a], corr, node_now[b][0:rows, a:a + 1], rows, ET * P - 1, cor_in[b])

            def gather_light(l):
                wait(pool, light_reset, l + 1)
                pool.sem_inc(gate, 1)
                g.tensor_copy(l_now[:], node_idx[:, bass.ds(l, 1)]).then_inc(light_now, 1)
                pool.wait_ge(light_now, l + 1)
                pool.sem_inc(gate, 1)
                gather(l_cor[:], corr, l_now[:, 0:1], P, ET * P - 1, light_cor_in)

            def light_make_rstd(l):
                wait(pool, light_mv, l + 1)
                wait(pool, light_shift, l)
                wait(pool, light_normed, l)
                pool.sem_inc(gate, 1)
                g.tensor_scalar(l_var_eps[:], l_mv[:, 1:2], EPS, None, ALU.add).then_inc(light_eps, 1)
                pool.wait_ge(light_eps, l + 1)
                g.tensor_tensor(l_rstd[:], l_var_eps[:], minus_half[:, 0:1], ALU.pow).then_inc(light_rstd, 1)

            def light(q, u):
                if u == 0:
                    light_at(q - 1, light_make_rstd)
                if u == 2:
                    light_at(q + 1, gather_light)

            def make_rstd(t, q, u):
                nt, rows = pair_shape(t)
                b = u % 2
                wait(pool, mv_made, 2 * t + 2)
                wait(pool, shift_made, t - 1)
                wait(pool, normed, t - 1)
                pool.sem_inc(gate, 1)
                g.tensor_scalar(var_eps[0:rows, b, 0:nt], mv[0:rows, b, 0:nt, 1], EPS, None, ALU.add
                                ).then_inc(eps_added, 1)
                pool.wait_ge(eps_added, t + 1)
                g.tensor_tensor(rstd[0:rows, b, 0:nt], var_eps[0:rows, b, 0:nt], minus_half[0:rows, 0:nt], ALU.pow
                                ).then_inc(rstd_made, 1)

            gather_light(0)
            single(0, gather_cor)
            single(1, gather_cor)

            def serve(t, q, u):
                shifted(t, q, u, 2, NP, gather_cor)
                shifted(t, q, u, -2, NP, make_rstd)
                light(q, u)
            steps(pool, NP, serve)
            for t in (NP - 2, NP - 1):
                single(t, make_rstd)
            light_tail(light)

        @block.tensor
        def _(pe):
            mm = nc.tensor.matmul
            pe.wait_ge(consts, 5)
            def three(ps, hi, lo, w_hi, w_lo):
                terms = [(a, w, k) for a, w in ((hi, w_hi), (hi, w_lo), (lo, w_hi)) for k in range(K)]
                for n, (a, w, k) in enumerate(terms):
                    last = mm(ps, a[:, k], w[:, k], start=(n == 0), stop=(n == len(terms) - 1))
                return last

            def transpose_early(t, q, u):
                b, used = ring(q, u, 2)
                pe.wait_ge(early_x_in[b], 16 * (used + 1))
                wait(pe, early_copied, t - 1)
                for k in range(K):
                    last = nc.tensor.transpose(pT[b][:, 0, k * P:(k + 1) * P], e_x[b][:, k * P:(k + 1) * P], eye)
                last.then_inc(early_transposed, 1)

            def early_tile(t, q, u):
                shifted(t, q, u, 1, EARLY, transpose_early)
                b = u % 2
                wait(pe, early_hi, t + 1)
                wait(pe, early_lo, t + 1)
                wait(pe, early_kept, t - 1)
                three(pH[0][:, b, :], x_hi[b][:, 0], x_lo[b][:, 0], ws_hi, ws_lo).then_inc(early_done, 1)
            single(0, transpose_early)
            pe.wait_ge(w_split, 1)
            peeled(0, 8, early_tile)
            pe.wait_ge(rows_moved, 1)
            for a in range(2):
                bank = pH[1][:, a, :]
                for c in range(CH):
                    mm(bank[:, c * P:(c + 1) * P], rowed_f[:, a * CH + c, P:2 * P], eye, start=(c == 0), stop=False)
                for c in range(CH):
                    lo = 1 if c == 0 else 0
                    last = mm(bank[:, c * P - 1 + lo:(c + 1) * P - 1], rowed_f[:, a * CH + c, 0:P],
                              eye[:, lo:P], start=False, stop=(c == CH - 1))
            last.then_inc(merged, 1)
            looped(pe, 2, 5, early_tile)
            pe.wait_ge(dst_found, 1)
            nc.tensor.transpose(t_dst_ps, dst_f[:, 1:1 + ET], eye)
            mm(t_before_ps, dst_f[:, 0:ET], eye[:, P - 1:P], start=True, stop=True).then_inc(t_ready, 1)
            pe.wait_ge(upto_ready, 1)
            mm(before_ps, eye3[:, P - 1:2 * P - 1], upto[:, 1:1 + NTILES], start=True, stop=False)
            mm(before_ps, eye3[:, 2 * P - 1:3 * P - 1], upto[:, 0:NTILES], start=False, stop=True
               ).then_inc(before_ready, 1)
            peeled(20, 21, early_tile)
            pe.wait_ge(t_scanned, 1)
            mm(ends_ps[:, 0:ET], t_run[0:ET, P - 1:P], eye[0:ET, 0:ET], start=True, stop=True)
            mm(ends_ps[:, ET:2 * ET], t_whole[0:ET, P - 1:P], eye[0:ET, 0:ET], start=True, stop=True
               ).then_inc(ends_ready, 1)
            peeled(21, 22, early_tile)
            pe.wait_ge(carry_ready, 1)
            mm(carry_ps, row_ends[0:1, 2, 0:ET], ones[0:1, 0:1], start=True, stop=True
               ).then_inc(carry_col, 1)
            peeled(22, 24, early_tile)
            pe.wait_ge(t_deg, 1)
            nc.tensor.transpose(rdeg_in_ps, t_rdeg[0:ET, :], eye[0:ET, 0:ET]).then_inc(rdeg_ps, 1)
            looped(pe, 6, EARLY // 4 - 1, early_tile)
            peeled(EARLY - 4, EARLY, early_tile)

            def spread(t, q, u):
                b = u % 2
                wait(pe, wide_made, t + 1)
                wait(pe, row_kept, t - 1)
                nc.tensor.transpose(pT[b][:, 1, 0:P], dst_wide[b][:], eye).then_inc(row_made, 1)

            def combine(t, q, u):
                b = u % 2
                wait(pe, sames_made, 2 * t + 2)
                wait(pe, diff_made, t + 1)
                wait(pe, sums_made, t - 1)
                for k in range(K):
                    last = mm(pT[b][:, 0, k * P:(k + 1) * P], diff[b][:, k * P:(k + 1) * P], same[b][:],
                              start=True, stop=True)
                last.then_inc(summed, 1)

            peeled(0, 3, spread)
            pe.wait_ge(early_copied, EARLY)
            single(0, combine)
            pe.wait_ge(rdeg_ready, 1)
            pe.wait_ge(early_kept, EARLY)
            pe.wait_ge(w_split, 1 + K)

            def edge_tile(t, q, u):
                shifted(t, q, u, 3, ET, spread)
                shifted(t, q, u, 1, ET, combine)
                b = u % 2
                wait(pe, s_hi_made, t + 1)
                wait(pe, s_lo_made, t + 1)
                wait(pe, c_made, t - 1)
                three(pH[b][:, 0, :], s_hi[b], s_lo[b], wl_hi, wl_lo).then_inc(c_product, 1)
            steps(pe, ET, edge_tile)

            def transpose_x(t, q, u):
                nt, rows = pair_shape(t)
                b, used = ring(q, u, 4)
                pe.wait_ge(x_in[b], 16 * (used + 1))
                wait(pe, lo_made, t - 1)
                for a in range(nt):
                    for k in range(K):
                        last = nc.tensor.transpose(pT[u % 2][:, a, k * P:k * P + rows],
                                                   X[0:rows, b, a, k * P:(k + 1) * P], eye[0:rows, 0:rows])
                last.then_inc(transposed, 1)

            pe.wait_ge(c_made, ET)
            single(0, transpose_x)

            def node_pair(t, q, u):
                shifted(t, q, u, 1, NP, transpose_x)
                nt, rows = pair_shape(t)
                b = u % 2
                wait(pe, hi_made, t + 1)
                wait(pe, lo_made, t + 1)
                wait(pe, z_made, t - 1)
                for a in range(nt):
                    last = three(pH[b][0:rows, a, :], x_hi[b][:, a, :, 0:rows], x_lo[b][:, a, :, 0:rows],
                                 ws_hi, ws_lo)
                last.then_inc(product, 1)
            steps(pe, NP, node_pair)

        @block.scalar
        def _(act):
            a_ = nc.scalar.activation
            act.preload_act_table_set("silu_and_others")
            act.wait_ge(weights_in, 32)
            act.wait_ge(w_summed, 1)
            a_(ws_hi[:], w_sum[:], ACT.Copy).then_inc(w_rounded, 1)

            def round_early(t, q, u):
                b = u % 2
                wait(act, early_transposed, t + 1)
                wait(act, early_done, t - 1)
                a_(x_hi[b][:, 0], pT[b][:, 0, :].rearrange("p (k r) -> p k r", k=K), ACT.Copy).then_inc(early_hi, 1)
                wait(act, early_lo, t - 1)
                a_(e_t[b][:], pT[b][:, 0, :], ACT.Copy).then_inc(early_copied, 1)

            def keep_early(t, q, u):
                b, used = ring(q, u, 2)
                wait(act, early_done, t + 1)
                wait(act, early_stored[b], 16 * used)
                a_(e_out[b][:], pH[0][:, b, :], ACT.Copy).then_inc(early_kept, 1)

            def early_tile(t, q, u):
                shifted(t, q, u, 1, EARLY, round_early)
                shifted(t, q, u, -1, EARLY, keep_early)
            single(0, round_early)
            a_(wl_hi[:], wl_raw[:], ACT.Copy).then_inc(w_rounded, 1)
            steps(act, EARLY, early_tile)
            single(EARLY - 1, keep_early)

            def widen(t, q, u):
                b = u % 2
                wait(act, row_made, t - 1)
                a_(dst_wide[b][:], dst_f[:, bass.ds(1 + t, 1)].to_broadcast([P, P]), ACT.Copy).then_inc(wide_made, 1)

            def keep_row(t, q, u):
                b = u % 2
                wait(act, row_made, t + 1)
                wait(act, row_kept, t)
                wait(act, sames_made, 2 * (t - 1))
                a_(dst_row[:, b, 1:1 + P], pT[b][:, 1, 0:P], ACT.Copy)
                if fixed(t) and t == 0:
                    a_(dst_row[:, b, 0:1], dst_f[:, 0:1], ACT.Copy).then_inc(row_kept, 1)
                else:
                    a_(dst_row[:, b, 0:1], dst_row[:, 1 - b, P:1 + P], ACT.Copy).then_inc(row_kept, 1)

            def round_sums(t, q, u):
                b = u % 2
                wait(act, sums_made, t + 1)
                wait(act, c_product, t - 1)
                a_(s_hi[b][:], sums[:, b], ACT.Copy).then_inc(s_hi_made, 1)

            act.wait_ge(dst_found, 1)
            for t in range(4):
                single(t, widen)
                if t < 3:
                    single(t, keep_row)
            single(0, round_sums)

            def edge_tile(t, q, u):
                shifted(t, q, u, 4, ET, widen)
                shifted(t, q, u, 3, ET, keep_row)
                shifted(t, q, u, 1, ET, round_sums)
            steps(act, ET, edge_tile)

            def round_x(t, q, u):
                nt, rows = pair_shape(t)
                b = u % 2
                wait(act, transposed, t + 1)
                wait(act, product, t - 1)
                a_(x_hi[b][:, 0:nt, :, 0:rows],
                   pT[b][:, 0:nt].rearrange("p a (k r) -> p a k r", k=K)[:, :, :, 0:rows], ACT.Copy).then_inc(hi_made, 1)

            def normalise(t, q, u):
                nt, rows = pair_shape(t)
                b, used = ring(q, u, 2)
                wait(act, shift_made, t + 1)
                wait(act, stored[b], 16 * used)
                for a in range(nt):
                    last = a_(O[0:rows, b, a], Z[0:rows, u % 4, a], ACT.Identity, scale=rstd[0:rows, b, a:a + 1],
                              bias=shift[0:rows, b, a:a + 1])
                last.then_inc(normed, 1)

            def silu(t, q, u):
                nt, rows = pair_shape(t)
                b = u % 4
                wait(act, z_made, t + 1)
                a_(Z[0:rows, b, 0:nt], Z[0:rows, b, 0:nt], ACT.Silu).then_inc(silu_made, 1)

            def reset_cor(t, q, u):
                wait(act, z_made, t - 3)
                a_(cor[u][:], bias_rows[:].rearrange("p (a n) -> p a n", a=1).to_broadcast([P, 2, D]), ACT.Copy
                   ).then_inc(cor_reset, 1)

            def reset_light(l):
                wait(act, light_z, l)
                a_(l_cor[:], bias_rows[:], ACT.Copy).then_inc(light_reset, 1)

            def light_make_silu(l):
                wait(act, light_z, l + 1)
                a_(l_z[:], l_z[:], ACT.Silu).then_inc(light_silu, 1)

            def light_normalise(l):
                wait(act, light_shift, l + 1)
                wait(act, light_stored, 16 * l)
                a_(l_o[:], l_u[:], ACT.Identity, scale=l_rstd[:, 0:1], bias=l_shift[:, 0:1]).then_inc(light_normed, 1)

            def light(q, u):
                if u == 1:
                    light_at(q - 1, light_normalise)
                if u == 2:
                    light_at(q, light_make_silu)
                    light_at(q + 1, reset_light)

            act.wait_ge(bias_in, 16)
            reset_light(0)
            single(0, reset_cor)
            single(1, reset_cor)
            single(0, round_x)

            def node_pair(t, q, u):
                shifted(t, q, u, 2, NP, reset_cor)
                shifted(t, q, u, 1, NP, round_x)
                shifted(t, q, u, -1, NP, silu)
                light(q, u)
                shifted(t, q, u, -3, NP, normalise)
            steps(act, NP, node_pair)
            single(NP - 1, silu)
            for t in range(NP - 3, NP):
                single(t, normalise)
            light_tail(light)

        @block.vector
        def _(dve):
            v = nc.vector
            done = [0]

            def then(ins):
                done[0] += 1
                ins.then_inc(dve_step, 1)
                dve.wait_ge(dve_step, done[0])

            v.memset(rowed[0], 0)
            then(v.memset(rowed[1], 0))
            dve.wait_ge(edges_in, 96)
            dve.wait_ge(pos_made, 2)
            v.tensor_tensor(e_rank, e_pos, e_dst, ALU.subtract)
            v.tensor_tensor(e_loop, e_dst, e_next, ALU.not_equal)
            then(v.tensor_tensor(e_other, e_dst, e_next, ALU.is_equal))
            v.tensor_tensor(rowed[0][:, 0:CH, P:], e_dst, e_other, ALU.mult)
            then(v.tensor_tensor(rowed[0][:, CH:, P:], e_rank, e_loop, ALU.mult))

            def move_left(out_, in_, mask, k, step, lo, hi, n):
                then(v.tensor_scalar(mask[:, :, lo:hi], in_[:, :, lo:hi], 31 - k, 31,
                                     ALU.logical_shift_left, ALU.arith_shift_right))
                then(v.scalar_tensor_tensor(out_[:, :, lo:hi], mask[:, :, lo:hi], -1, in_[:, :, lo:hi],
                                            ALU.bitwise_xor, ALU.bitwise_and))
                to = max(lo - step, 0)
                then(v.copy_predicated(out_[:, :, to:hi - step], mask[:, :, to + step:hi], in_[:, :, to + step:hi]))

            for k in range(ROW_BITS):
                move_left(rowed[(k + 1) % 2], rowed[k % 2], row_mask, k, 1 << k, P - (1 << k) + 1, 2 * P, None)
            then(v.tensor_copy(rowed_f[:], rowed[ROW_BITS % 2]))
            dve.sem_inc(rows_moved, 1)
            dve.wait_ge(merged, 1)
            then(v.tensor_copy(col[0], pH[1][:]))
            for k in range(ROW_BITS, BITS):
                n = k - ROW_BITS
                move_left(col[(n + 1) % 2], col[n % 2], col_mask, k, 1 << n, 0, COLS, None)
            found = col[(BITS - ROW_BITS) % 2]
            v.tensor_copy(dst_c, found[:, 0, 0:ET]).then_inc(dst_ready, 1)
            v.memset(upto[:, 0:1], 0.0)
            v.tensor_copy(upto[:, 1:1 + NTILES], found[:, 1, 0:NTILES]).then_inc(upto_ready, 1)
            dve.wait_ge(dst_padded, 1)
            then(v.tensor_tensor(edge_idx[:, :, 0], dst_c, r_pos, ALU.add))
            v.tensor_scalar(edge_idx[:, :, 0], edge_idx[:, :, 0], E - 1.0, None, ALU.min)
            v.tensor_scalar(edge_idx[:, :, 1], dst_c, N - 1.0, None, ALU.min)
            then(v.tensor_copy(dst_f[:, 1:1 + ET], dst_c))
            dve.sem_inc(dst_found, 1)
            dve.wait_ge(consts, 5)
            dve.wait_ge(t_ready, 1)
            v.tensor_copy(t_dst[0:ET, 1:1 + P], t_dst_ps)
            then(v.tensor_copy(t_dst[0:ET, 0:1], t_before_ps))
            then(v.tensor_tensor(t_same[0:ET], t_dst[0:ET, 1:1 + P], t_dst[0:ET, 0:P], ALU.is_equal))
            v.tensor_tensor_scan(t_run[0:ET], t_same[0:ET], ones[0:ET, :], 0.0, ALU.mult, ALU.add)
            v.tensor_tensor_scan(t_whole[0:ET], t_same[0:ET], zeros[0:ET, :], 1.0, ALU.mult, ALU.add
                                 ).then_inc(t_scanned, 1)
            dve.wait_ge(before_ready, 1)
            then(v.tensor_tensor(none, upto[:, 1:1 + NTILES], before_ps, ALU.subtract))
            then(v.tensor_scalar(none, none, 0.0, float(SKIP), ALU.is_equal, ALU.mult))
            v.memset(node_idx[:, NTILES:NTILES + 1], SKIP)
            v.scalar_tensor_tensor(node_idx[:, 0:NTILES], upto[:, 1:1 + NTILES], -1.0, none, ALU.add, ALU.add
                                   ).then_inc(idx_ready, 1)
            dve.wait_ge(ends_ready, 1)
            v.memset(row_ends[0:1, 2, 0:1], 0.0)
            then(v.tensor_copy(row_ends[0:1, 0:2, 0:ET],
                               ends_ps.rearrange("p (a c) -> p a c", a=2)))
            v.tensor_tensor_scan(row_ends[0:1, 2, 1:ET], row_ends[0:1, 1, 0:ET - 1], row_ends[0:1, 0, 0:ET - 1], 0.0,
                                 ALU.mult, ALU.add).then_inc(carry_ready, 1)
            dve.wait_ge(carry_col, 1)
            then(v.scalar_tensor_tensor(t_count[0:ET], t_whole[0:ET], carry_ps, t_run[0:ET],
                                        ALU.mult, ALU.add))
            then(v.tensor_scalar(t_count[0:ET], t_count[0:ET], 1.0, None, ALU.add))
            v.reciprocal(t_rdeg[0:ET], t_count[0:ET]).then_inc(t_deg, 1)
            dve.wait_ge(rdeg_ps, 1)
            then(v.tensor_copy(rdeg[:], rdeg_in_ps))
            dve.sem_inc(rdeg_ready, 1)
            dve.wait_ge(bias_in, 16)

            def compare(t, q, u):
                b = u % 2
                r, used = ring(q, u, 4)
                wait(dve, row_kept, t + 1)
                wait(dve, summed, t - 1)
                v.tensor_scalar(same[b][:], dst_row[:, b, 1:1 + P], dst_f[:, bass.ds(1 + t, 1)], None, ALU.is_equal
                                ).then_inc(sames_made, 1)
                v.tensor_scalar(goes_on[:, b], dst_row[:, b, 1:1 + P], dst_row[:, b, 0:1], None, ALU.is_equal
                                ).then_inc(sames_made, 1)
                dve.wait_ge(xs_in[r], 16 * (used + 1))
                dve.wait_ge(xd_in[r], 16 * (used + 1))
                v.tensor_tensor(diff[b][:], xs[r][:], xd[r][:], ALU.subtract).then_inc(diff_made, 1)

            def carry(t, q, u):
                b = u % 2
                wait(dve, summed, t + 1)
                wait(dve, sums_made, t)
                wait(dve, s_lo_made, t - 1)
                wait(dve, s_hi_made, t - 1)
                for k in range(K):
                    last = v.scalar_tensor_tensor(
                        sums[:, b, k], goes_on[:, b], zeros[:, 0:1] if fixed(t) and t == 0 else sums[:, 1 - b, k, P - 1:P],
                        pT[b][:, 0, k * P:(k + 1) * P], ALU.mult, ALU.add)
                last.then_inc(sums_made, 1)

            def split_sums(t, q, u):
                b = u % 2
                wait(dve, s_hi_made, t + 1)
                wait(dve, c_product, t - 1)
                v.tensor_tensor(s_lo[b][:], sums[:, b], s_hi[b][:].bitcast(f32), ALU.subtract).then_inc(s_lo_made, 1)

            def finish(t, q, u):
                b, used = ring(q, u, 2)
                wait(dve, c_product, t + 1)
                wait(dve, c_stored[b], 16 * used)
                v.scalar_tensor_tensor(c_out[:, b], pH[b][:, 0, :], rdeg[:, bass.ds(t, 1)], bias_rows[:],
                                       ALU.mult, ALU.add).then_inc(c_made, 1)

            single(0, compare)
            single(0, carry)
            single(1, compare)
            single(0, split_sums)

            def edge_tile(t, q, u):
                shifted(t, q, u, -1, ET, finish)
                shifted(t, q, u, 1, ET, carry)
                shifted(t, q, u, 2, ET, compare)
                shifted(t, q, u, 1, ET, split_sums)
            steps(dve, ET, edge_tile)
            single(ET - 1, finish)

            def split_x(t, q, u):
                nt, rows = pair_shape(t)
                b = u % 2
                wait(dve, hi_made, t + 1)
                v.tensor_tensor(x_lo[b][:, 0:nt, :, 0:rows],
                                pT[b][:, 0:nt].rearrange("p a (k r) -> p a k r", k=K)[:, :, :, 0:rows],
                                x_hi[b][:, 0:nt, :, 0:rows].bitcast(f32), ALU.subtract).then_inc(lo_made, 1)

            def add_cor(t, q, u):
                nt, rows = pair_shape(t)
                b, used = ring(q, u, 4)
                wait(dve, product, t + 1)
                if nt == 2:
                    dve.wait_ge(cor_in[b], 32 * (used + 1))
                else:
                    dve.wait_ge(cor_in[b], 32 * used + 16)
                wait(dve, normed, t - 3)
                v.tensor_tensor(Z[0:rows, b, 0:nt], pH[u % 2][0:rows, 0:nt], cor[b][0:rows, 0:nt], ALU.add
                                ).then_inc(z_made, 1)

            def residual(t, q, u):
                nt, rows = pair_shape(t)
                b = u % 4
                wait(dve, silu_made, t + 1)
                v.tensor_tensor(Z[0:rows, b, 0:nt], Z[0:rows, b, 0:nt], X[0:rows, b, 0:nt], ALU.add
                                ).then_inc(u_made, 1)

            def moments(t, q, u):
                nt, rows = pair_shape(t)
                wait(dve, u_made, t + 1)
                wait(dve, rstd_made, t - 1)
                for a in range(nt):
                    v.bn_stats(stats[0:rows, u % 2, a], Z[0:rows, u % 4, a]).then_inc(stats_made, 1)
                wait(dve, stats_made, 2 * t + nt)
                dve.sem_inc(dve_gate, 1)
                for a in range(nt):
                    v.bn_aggr(mv[0:rows, u % 2, a], stats[0:rows, u % 2, a]).then_inc(mv_made, 3 - nt)

            def make_shift(t, q, u):
                nt, rows = pair_shape(t)
                b = u % 2
                wait(dve, rstd_made, t + 1)
                wait(dve, normed, t - 1)
                v.scalar_tensor_tensor(shift[0:rows, b, 0:nt], mv[0:rows, b, 0:nt, 0], -1.0, rstd[0:rows, b, 0:nt],
                                       ALU.mult, ALU.mult).then_inc(shift_made, 1)

            def light_add(l):
                dve.wait_ge(light_in, 32 * (l + 1))
                dve.wait_ge(light_cor_in, 16 * (l + 1))
                v.tensor_tensor(l_z[:], l_h[:], l_cor[:], ALU.add).then_inc(light_z, 1)

            def light_residual(l):
                wait(dve, light_silu, l + 1)
                wait(dve, light_normed, l)
                v.tensor_tensor(l_u[:], l_z[:], l_x[:], ALU.add).then_inc(light_u, 1)

            def light_moments(l):
                wait(dve, light_u, l + 1)
                wait(dve, light_rstd, l)
                v.bn_stats(l_stats[:], l_u[:]).then_inc(light_stats, 1)
                wait(dve, light_stats, l + 1)
                dve.sem_inc(dve_gate, 1)
                v.bn_aggr(l_mv[:], l_stats[:]).then_inc(light_mv, 1)

            def light_make_shift(l):
                wait(dve, light_rstd, l + 1)
                wait(dve, light_normed, l)
                v.scalar_tensor_tensor(l_shift[:], l_mv[:, 0:1], -1.0, l_rstd[:], ALU.mult, ALU.mult
                                       ).then_inc(light_shift, 1)

            def light(q, u):
                if u == 0:
                    light_at(q - 1, light_make_shift)
                if u == 1:
                    light_at(q, light_add)
                if u == 2:
                    light_at(q, light_residual)
                if u == 3:
                    light_at(q, light_moments)

            single(0, split_x)

            def node_pair(t, q, u):
                shifted(t, q, u, -1, NP, add_cor)
                shifted(t, q, u, -2, NP, moments)
                shifted(t, q, u, 1, NP, split_x)
                shifted(t, q, u, -1, NP, residual)
                shifted(t, q, u, -2, NP, make_shift)
                light(q, u)
            steps(dve, NP, node_pair)
            single(NP - 1, add_cor)
            single(NP - 2, moments)
            single(NP - 1, residual)
            single(NP - 2, make_shift)
            single(NP - 1, moments)
            single(NP - 1, make_shift)
            light_tail(light)


_INS = ["x", "src", "dst", "L0_gnn_W_l", "L0_gnn_W_r", "L0_gnn_b"]


def kernel(**inputs):
    import numpy as _np
    import concourse.bacc as _bacc
    from concourse import mybir as _mybir
    from concourse.bass_utils import run_bass_kernel_spmd as _run

    nc = _bacc.Bacc("TRN2", target_bir_lowering=False, num_devices=1)
    arrays, args = {}, []
    for name in _INS:
        a = _np.ascontiguousarray(inputs[name])
        arrays[f"in_{name}"] = a
        args.append(nc.dram_tensor(f"in_{name}", a.shape, _mybir.dt.from_np(a.dtype), kind="ExternalInput").ap())
    shape = tuple(inputs["x"].shape)
    args.append(nc.dram_tensor("out_0", shape, _mybir.dt.float32, kind="ExternalOutput").ap())
    gnn_layer(nc, *args)
    r = _run(nc, [arrays], core_ids=[0])
    return r.results[0]["out_0"]
```

```python
from contextlib import ExitStack

import concourse.bass as bass
from concourse import mybir


def gnn_layer(nc, x, src, dst, w_l, w_r, bias, out):
    f32, f32r, i32 = mybir.dt.float32, mybir.dt.float32r, mybir.dt.int32
    ALU = mybir.AluOpType
    ACT = mybir.ActivationFunctionType
    P = nc.NUM_PARTITIONS

    N, D = x.shape
    E = src.shape[0]
    R = E - N
    K = D // P
    EPS = 1e-5

    EDGE_ROWS, EDGE_TAIL = E // P, E % P
    CH = -(-(EDGE_ROWS + 1) // P)
    FULL = (CH - 1) * P
    COLS = CH * P
    ROW_BITS = P.bit_length() - 1
    BITS = (N - 1).bit_length()
    ET = -(-R // P)
    R_LAST = R - (ET - 1) * P
    NTILES = -(-N // P)
    N_LAST = N - (NTILES - 1) * P
    EARLY = 44
    BASE = EARLY * P
    NP = -(-(NTILES - EARLY) // 2)
    MERGE_ROUND, FIND_ROUND = 4, 7
    SKIP = 1 << 20
    assert (NTILES - EARLY) % 2 == 1 and ET % 2 == 0 and NP % 2 == 0 and COLS <= 512
    assert EARLY - 1 == NP // 4
    assert BITS - ROW_BITS <= COLS.bit_length()

    corr = nc.dram_tensor("correction_rows", (ET * P, D), f32, kind="Internal").ap()
    early_product = nc.dram_tensor("early_product", (BASE, D), f32, kind="Internal").ap()
    dst_list = nc.dram_tensor("dst_list", (1 + ET * P,), f32, kind="Internal").ap()
    src_rows = src.rearrange("(e a) -> e a", a=1)

    ctx = ExitStack()
    with ctx:
        def sb(name, shape, dt):
            return ctx.enter_context(nc.sbuf_tensor(name, shape, dt))

        def sem(name):
            return ctx.enter_context(nc.semaphore(name))

        eye3 = sb("eye3", [P, 3 * P], f32)
        eye = eye3[:, P:2 * P]
        ones = sb("ones", [P, P], f32)
        zeros = sb("zeros", [P, P], f32)
        minus_half = sb("minus_half", [P, 2], f32)
        bias_rows = sb("bias_rows", [P, D], f32)
        wl_raw = sb("wl_raw", [P, K, D], f32)
        wr_raw = sb("wr_raw", [P, K, D], f32)
        w_sum = sb("w_sum", [P, K, D], f32)
        ws_hi, ws_lo = sb("ws_hi", [P, K, D], f32r), sb("ws_lo", [P, K, D], f32r)
        wl_hi, wl_lo = sb("wl_hi", [P, K, D], f32r), sb("wl_lo", [P, K, D], f32r)
        X = sb("X", [P, 4, 2, D], f32)
        x_hi = [sb(f"x_hi{b}", [P, 2, K, P], f32r) for b in range(2)]
        x_lo = [sb(f"x_lo{b}", [P, 2, K, P], f32r) for b in range(2)]
        cor = [sb(f"cor{b}", [P, 2, D], f32) for b in range(4)]
        Z = sb("Z", [P, 4, 2, D], f32)
        O = sb("O", [P, 2, 2, D], f32)
        stats = sb("stats", [P, 2, 2, nc.vector.BN_STATS_DIM], f32)
        mv = sb("mv", [P, 2, 2, 2], f32)
        var_eps = sb("var_eps", [P, 2, 2], f32)
        rstd = sb("rstd", [P, 2, 2], f32)
        shift = sb("shift", [P, 2, 2], f32)
        node_idx = sb("node_idx", [P, NTILES + 1], i32)
        node_now = [sb(f"node_now{b}", [P, 2], i32) for b in range(4)]
        l_x, l_h, l_cor, l_z, l_u, l_o = (sb(f"light_{n}", [P, D], f32) for n in ("x", "h", "cor", "z", "u", "o"))
        l_stats, l_mv = sb("l_stats", [P, nc.vector.BN_STATS_DIM], f32), sb("l_mv", [P, 2], f32)
        l_var_eps, l_rstd, l_shift = sb("l_var_eps", [P, 1], f32), sb("l_rstd", [P, 1], f32), sb("l_shift", [P, 1], f32)
        l_now = sb("l_now", [P, 1], i32)
        e_x, e_t, e_out = (l_x, l_h), (l_cor, l_z), (l_u, l_o)
        edge_idx = sb("edge_idx", [P, ET, 2], i32)
        dst_f = sb("dst_f", [P, 1 + ET], f32)
        rdeg = sb("rdeg", [P, ET], f32)
        edge_now = [sb(f"edge_now{b}", [P, 2], i32) for b in range(4)]
        src_now = [sb(f"src_now{b}", [P, 1], i32) for b in range(4)]
        xs = [sb(f"xs{b}", [P, D], f32) for b in range(4)]
        xd = [sb(f"xd{b}", [P, D], f32) for b in range(4)]
        diff = [sb(f"diff{b}", [P, D], f32) for b in range(2)]
        dst_row = sb("dst_row", [P, 4, 1 + P], f32)
        same = [sb(f"same{b}", [P, P], f32) for b in range(2)]
        goes_on = sb("goes_on", [P, 2, P], f32)
        sums = sb("sums", [P, 2, K, P], f32)
        s_hi = [sb(f"s_hi{b}", [P, K, P], f32r) for b in range(2)]
        s_lo = [sb(f"s_lo{b}", [P, K, P], f32r) for b in range(2)]
        c_out = sb("c_out", [P, 2, D], f32)
        Xi = X[:].bitcast(i32)
        rowed = [Xi[:, 2 * b:2 * b + 2].rearrange("p a t (c j) -> p (a t c) j", j=2 * P) for b in range(2)]
        assert 2 * CH * 2 * P <= 2 * 2 * D
        row_mask = sb("row_mask", [P, 2 * CH, 2 * P], i32)
        rowed_f = sb("rowed_f", [P, 2 * CH, 2 * P], f32)
        col = [cor[b][:].bitcast(i32) for b in range(2)]
        col_mask = cor[2][:].bitcast(i32)
        e_dst = cor[3][:, 0].bitcast(i32).rearrange("p (c j) -> p c j", j=P)
        e_next = cor[3][:, 1].bitcast(i32).rearrange("p (c j) -> p c j", j=P)
        e_pos = Z[:, 0, 0].bitcast(i32).rearrange("p (c j) -> p c j", j=P)
        e_other = Z[:, 0, 1].bitcast(i32).rearrange("p (c j) -> p c j", j=P)
        e_loop = Z[:, 1, 0].bitcast(i32).rearrange("p (c j) -> p c j", j=P)
        e_rank = Z[:, 1, 1].bitcast(i32).rearrange("p (c j) -> p c j", j=P)
        upto = O[:, 0, 0, 0:1 + NTILES]
        none = O[:, 0, 1, 0:NTILES]
        r_pos = O[:, 1, 0, 0:ET].bitcast(i32)
        dst_c = O[:, 1, 0, P:P + ET].bitcast(i32)
        t_dst = O[:, 1, 1, 0:1 + P]
        t_same = O[:, 1, 1, P + 16:P + 16 + P]
        t_run = sums[:, 0, 0]
        t_whole = sums[:, 0, 1]
        t_count = sums[:, 0, 2]
        t_rdeg = sums[:, 0, 3]
        row_ends = sb("row_ends", [1, 3, P], f32)

        pT = [ctx.enter_context(nc.psum_tensor(f"pT{b}", [P, 2, D], f32)) for b in range(2)]
        pH = [ctx.enter_context(nc.psum_tensor(f"pH{b}", [P, 2, D], f32)) for b in range(2)]

        before_ps = pH[1][:, 0, 0:NTILES]
        t_dst_ps = pH[1][0:ET, 1, 0:P]
        t_before_ps = pH[1][0:ET, 1, P:P + 1]
        carry_ps = pH[1][0:ET, 1, P + 4:P + 5]
        ends_ps = pH[1][0:1, 1, P + 8:P + 8 + 2 * ET]
        rdeg_in_ps = pH[1][:, 1, 3 * P:3 * P + ET]

        pads_zero, edges_in, bias_in, weights_in = sem("pads_zero"), sem("edges_in"), sem("bias_in"), [sem(f"weights_in{k}") for k in range(K)]
        eye_clear, consts, pos_made = sem("eye_clear"), sem("consts"), sem("pos_made")
        w_summed, ws_rounded, ws_split = sem("w_summed"), sem("ws_rounded"), sem("ws_split")
        wl_rounded, wl_split = sem("wl_rounded"), sem("wl_split")
        dve_step, rows_moved, merged = sem("dve_step"), sem("rows_moved"), sem("merged")
        dst_padded, dst_ready, dst_found = sem("dst_padded"), sem("dst_ready"), sem("dst_found")
        upto_ready, before_ready = sem("upto_ready"), sem("before_ready")
        t_ready, t_scanned, ends_ready = sem("t_ready"), sem("t_scanned"), sem("ends_ready")
        carry_ready, carry_col, t_deg, rdeg_ps, rdeg_ready = (sem("carry_ready"), sem("carry_col"), sem("t_deg"),
                                                             sem("rdeg_ps"), sem("rdeg_ready"))
        idx_ready = sem("idx_ready")
        gate, dve_gate = sem("gate"), sem("dve_gate")
        now_copied = sem("now_copied")
        src_in = [sem(f"src_in{b}") for b in range(4)]
        xs_in = [sem(f"xs_in{b}") for b in range(4)]
        xd_in = [sem(f"xd_in{b}") for b in range(4)]
        list_made, list_stored = sem("list_made"), sem("list_stored")
        row_in = [sem(f"row_in{b}") for b in range(4)]
        sames_made, diff_made = sem("sames_made"), sem("diff_made")
        summed, sums_made, s_hi_made, s_lo_made, c_product, c_made = (sem("summed"), sem("sums_made"),
                                                                     sem("s_hi_made"), sem("s_lo_made"),
                                                                     sem("c_product"), sem("c_made"))
        c_stored = [sem(f"c_stored{b}") for b in range(2)]
        x_in = [sem(f"x_in{b}") for b in range(4)]
        cor_in = [sem(f"cor_in{b}") for b in range(4)]
        transposed, hi_made, lo_made, product, z_made, silu_made = (sem("transposed"), sem("hi_made"), sem("lo_made"),
                                                                   sem("product"), sem("z_made"), sem("silu_made"))
        u_made, stats_made, mv_made, eps_added, rstd_made, shift_made, normed = (
            sem("u_made"), sem("stats_made"), sem("mv_made"), sem("eps_added"), sem("rstd_made"),
            sem("shift_made"), sem("normed"))
        cor_reset, node_ready = sem("cor_reset"), sem("node_ready")
        stored = [sem(f"stored{b}") for b in range(2)]

        early_x_in = [sem(f"early_x_in{b}") for b in range(2)]
        early_stored = [sem(f"early_stored{b}") for b in range(2)]
        early_transposed, early_hi, early_copied, early_lo, early_done, early_kept = (
            sem("early_transposed"), sem("early_hi"), sem("early_copied"), sem("early_lo"),
            sem("early_done"), sem("early_kept"))
        light_in, light_now, light_reset, light_cor_in, light_z, light_silu, light_u = (
            sem("light_in"), sem("light_now"), sem("light_reset"), sem("light_cor_in"), sem("light_z"),
            sem("light_silu"), sem("light_u_made"))
        light_stats, light_mv, light_eps, light_rstd, light_shift, light_normed, light_stored = (
            sem("light_stats"), sem("light_mv"), sem("light_eps"), sem("light_rstd_made"),
            sem("light_shift"), sem("light_normed"), sem("light_stored"))

        block = ctx.enter_context(nc.Block())

        def fixed(v):
            return isinstance(v, int)

        def wait(eng, s, v):
            if not fixed(v) or v > 0:
                eng.wait_ge(s, v)

        def steps(eng, n, step):
            rounds = n // 4
            peeled(0, 8, step)
            looped(eng, 2, rounds - 1, step)
            peeled(4 * (rounds - 1), n, step)

        def peeled(first, end, step):
            for t in range(first, end):
                step(t, t // 4, t % 4)

        def looped(eng, first, end, step):
            with eng.Fori(first, end) as q:
                for u in range(4):
                    step(4 * q + u, q, u)

        def light_tail(light, first, end):
            for k in range(first, end):
                light(k // 4, k % 4)

        def light_at(l, step):
            if not fixed(l) or 0 <= l < EARLY:
                step(l)

        def shifted(t, q, u, by, n, step):
            if not fixed(t) or 0 <= t + by < n:
                step(t + by, q + (u + by) // 4, (u + by) % 4)

        def single(t, step):
            step(t, t // 4, t % 4)

        def ring(q, u, n):
            return u % n, q * (4 // n) + u // n

        def pair_shape(j):
            return (1, N_LAST) if fixed(j) and j == NP - 1 else (2, P)

        @block.sync
        def _(sp):
            def load_early(t, q, u):
                b = u % 2
                wait(sp, early_transposed, t - 1)
                sp.dma_start(e_x[b][:], x[bass.ts(t, P), :]).then_inc(early_x_in[b], 16)

            def store_early(t, q, u):
                b = u % 2
                wait(sp, early_kept, t + 1)
                sp.dma_start(early_product[bass.ts(t, P), :], e_out[b][:]).then_inc(early_stored[b], 16)

            def move_early(t, q, u):
                shifted(t, q, u, 2, EARLY, load_early)
                shifted(t, q, u, -1, EARLY, store_early)
            single(0, load_early)
            for k in range(K):
                sp.dma_start(wl_raw[:, k], w_l[k * P:(k + 1) * P, :]).then_inc(weights_in[k], 16)
                sp.dma_start(wr_raw[:, k], w_r[k * P:(k + 1) * P, :]).then_inc(weights_in[k], 16)
            single(1, load_early)
            sp.dma_start(bias_rows[:], bias.rearrange("(a n) -> a n", a=1).to_broadcast([P, D])).then_inc(bias_in, 16)

            def load_row(t, q, u):
                wait(sp, sames_made, 2 * (t - 3))
                sp.dma_start(dst_row[:, u], dst_list[bass.ds(t * P, 1 + P)].rearrange("(a e) -> a e", a=1)
                             .to_broadcast([P, 1 + P])).then_inc(row_in[u], 16)

            peeled(0, 8, move_early)
            looped(sp, 2, EARLY // 4 - 2, move_early)
            sp.wait_ge(list_made, 1)
            sp.dma_start(dst_list[0:1].rearrange("(a e) -> a e", a=1), t_dst[0:1, 0:1]).then_inc(list_stored, 16)
            sp.dma_start(dst_list[1:1 + ET * P].rearrange("(t e) -> t e", e=P), t_dst[0:ET, 1:1 + P]
                         ).then_inc(list_stored, 16)
            peeled(EARLY - 8, EARLY - 4, move_early)
            sp.wait_ge(list_stored, 32)
            for t in range(4):
                single(t, load_row)
            peeled(EARLY - 4, EARLY, move_early)
            single(EARLY - 1, store_early)

            def store_c(t, q, u):
                b = u % 2
                wait(sp, c_made, t + 1)
                sp.dma_start(corr[bass.ts(t, P), :], c_out[:, b]).then_inc(c_stored[b], 16)

            def load_x(t, q, u):
                nt, rows = pair_shape(t)
                b, used = ring(q, u, 4)
                wait(sp, u_made, t - 3)
                if nt == 2:
                    sp.dma_start(X[:, b], x[bass.ds(BASE + t * 2 * P, 2 * P), :].rearrange("(a p) n -> p a n", p=P)
                                 ).then_inc(x_in[b], 16)
                else:
                    sp.dma_start(X[0:rows, b, 0], x[BASE + t * 2 * P:N, :]).then_inc(x_in[b], 16)

            def store_out(t, q, u):
                nt, rows = pair_shape(t)
                b = u % 2
                wait(sp, normed, t + 1)
                if nt == 2:
                    sp.dma_start(out[bass.ds(BASE + t * 2 * P, 2 * P), :].rearrange("(a p) n -> p a n", p=P), O[:, b]
                                 ).then_inc(stored[b], 16)
                else:
                    sp.dma_start(out[BASE + t * 2 * P:N, :], O[0:rows, b, 0]).then_inc(stored[b], 16)

            def load_light(l):
                wait(sp, light_u, l)
                sp.dma_start(l_x[:], x[bass.ts(l, P), :]).then_inc(light_in, 16)
                sp.dma_start(l_h[:], early_product[bass.ts(l, P), :]).then_inc(light_in, 16)

            def store_light(l):
                wait(sp, light_normed, l + 1)
                sp.dma_start(out[bass.ts(l, P), :], l_o[:]).then_inc(light_stored, 16)

            def light(q, u):
                if u == 2:
                    light_at(q - 1, store_light)
                if u == 3:
                    light_at(q + 1, load_light)
            sp.wait_ge(rows_moved, 1)
            for b in range(2):
                sp.wait_ge(early_stored[b], 16 * (EARLY // 2))

            def edge_tile(t, q, u):
                shifted(t, q, u, 4, ET, load_row)
                store_c(t, q, u)
                if fixed(t) and ET - 6 <= t < ET - 3:
                    single(t - (ET - 6), load_x)
                if fixed(t) and t == ET - 3:
                    load_light(0)
            steps(sp, ET, edge_tile)

            def move(t, q, u):
                shifted(t, q, u, 3, NP, load_x)
                shifted(t, q, u, -3, NP, store_out)
                light(q, u)
            steps(sp, NP, move)
            light_tail(light, NP, 4 * EARLY)
            for t in range(NP - 3, NP):
                single(t, store_out)
            light_tail(light, 4 * EARLY, 4 * EARLY + 4)
            sp.wait_ge(light_stored, 16 * EARLY)
            for b in range(2):
                sp.wait_ge(stored[b], 16 * (NP // 2))

        @block.gpsimd
        def _(pool):
            g = nc.gpsimd
            g.memset(e_dst[:, CH - 1], 0).then_inc(pads_zero, 1)
            g.memset(e_next[:, CH - 1], 0).then_inc(pads_zero, 1)
            g.iota(e_pos, [[P * P, CH], [1, P]], base=0, channel_multiplier=P).then_inc(pos_made, 1)
            g.iota(r_pos, [[P, ET]], base=0, channel_multiplier=1).then_inc(pos_made, 1)
            g.memset(eye3[:], 0.0).then_inc(eye_clear, 1)
            pool.wait_ge(eye_clear, 1)
            g.affine_select(out=eye3[:], in_=eye3[:], compare_op=ALU.not_equal, fill=1.0, base=P,
                            pattern=[[-1, 3 * P]], channel_multiplier=1).then_inc(consts, 1)
            g.memset(ones[:], 1.0).then_inc(consts, 1)
            g.memset(zeros[:], 0.0).then_inc(consts, 1)
            g.memset(minus_half[:], -0.5).then_inc(consts, 1)
            g.memset(dst_f[:, 0:1], -1.0).then_inc(consts, 1)

            def split_early(t, q, u):
                b = u % 2
                wait(pool, early_copied, t + 1)
                wait(pool, early_done, t - 1)
                g.tensor_tensor(x_lo[b][:, 0], e_t[b][:].rearrange("p (k r) -> p k r", k=K),
                                x_hi[b][:, 0].bitcast(f32), ALU.subtract).then_inc(early_lo, 1)
            peeled(0, 4, split_early)
            pool.wait_ge(wl_rounded, 1)
            for k in range(K):
                g.tensor_tensor(wl_lo[:, k], wl_raw[:, k], wl_hi[:, k].bitcast(f32), ALU.subtract
                                ).then_inc(wl_split, 1)
                single(4 + k, split_early)
            looped(pool, 2, FIND_ROUND, split_early)
            pool.wait_ge(dst_ready, 1)
            g.affine_select(out=dst_c[:, ET - 1:ET], in_=dst_c[:, ET - 1:ET], compare_op=ALU.is_ge,
                            fill=float(N), base=R_LAST - 1, pattern=[[0, 1]], channel_multiplier=-1
                            ).then_inc(dst_padded, 1)
            looped(pool, FIND_ROUND, EARLY // 4 - 3, split_early)

            def gather(out_, table, idx, rows, bound, s):
                g.indirect_dma_start(out=out_, out_offset=None, in_=table,
                                     in_offset=bass.IndirectOffsetOnAxis(ap=idx, axis=0),
                                     bounds_check=bound, oob_is_err=False).then_inc(s, 16)

            def gather_src(t, q, u):
                b, used = ring(q, u, 4)
                if not fixed(t) or t > 3:
                    wait(pool, diff_made, t - 3)
                    pool.sem_inc(gate, 1)
                g.tensor_copy(edge_now[b][:], edge_idx[:, bass.ds(t, 1)].rearrange("p t a -> p (t a)")
                              ).then_inc(now_copied, 1)
                pool.wait_ge(now_copied, t + 1)
                pool.sem_inc(gate, 1)
                gather(src_now[b][:], src_rows, edge_now[b][:, 0:1], P, E - 1, src_in[b])

            def gather_xd(t, q, u):
                gather(xd[u][:], x, edge_now[u][:, 1:2], P, N - 1, xd_in[u])

            def gather_xs(t, q, u):
                b, used = ring(q, u, 4)
                pool.wait_ge(src_in[b], 16 * (used + 1))
                pool.sem_inc(gate, 1)
                gather(xs[b][:], x, src_now[b][:, 0:1], P, N - 1, xs_in[b])

            def gather_edges(t, q, u):
                gather_src(t, q, u)
                gather_xd(t, q, u)
                shifted(t, q, u, -1, ET, gather_xs)

            peeled(EARLY - 12, EARLY - 9, split_early)
            pool.wait_ge(dst_found, 1)
            for e in range(3):
                for n, fetch in enumerate((gather_src, gather_xd, gather_xs)):
                    single(EARLY - 9 + 3 * e + n, split_early)
                    single(e, fetch)
            single(3, gather_src)
            single(3, gather_xd)
            peeled(4, 8, gather_edges)
            looped(pool, 2, ET // 4 - 1, gather_edges)
            peeled(4 * (ET // 4 - 1), ET, gather_edges)
            single(ET - 1, gather_xs)

            for b in range(2):
                pool.wait_ge(c_stored[b], 16 * (ET // 2))
            pool.wait_ge(idx_ready, 1)

            def gather_cor(t, q, u):
                nt, rows = pair_shape(t)
                b, used = ring(q, u, 4)
                wait(pool, cor_reset, t + 1)
                pool.sem_inc(gate, 1)
                g.tensor_copy(node_now[b][:, 0:nt], node_idx[:, bass.ds(EARLY + 2 * t, nt)]).then_inc(node_ready, 1)
                pool.wait_ge(node_ready, t + 1)
                pool.sem_inc(gate, 1)
                for a in range(nt):
                    gather(cor[b][0:rows, a], corr, node_now[b][0:rows, a:a + 1], rows, ET * P - 1, cor_in[b])

            def gather_light(l):
                wait(pool, light_reset, l + 1)
                pool.sem_inc(gate, 1)
                g.tensor_copy(l_now[:], node_idx[:, bass.ds(l, 1)]).then_inc(light_now, 1)
                pool.wait_ge(light_now, l + 1)
                pool.sem_inc(gate, 1)
                gather(l_cor[:], corr, l_now[:, 0:1], P, ET * P - 1, light_cor_in)

            def light_make_rstd(l):
                wait(pool, light_mv, l + 1)
                wait(pool, light_shift, l)
                wait(pool, light_normed, l)
                pool.sem_inc(gate, 1)
                g.tensor_scalar(l_var_eps[:], l_mv[:, 1:2], EPS, None, ALU.add).then_inc(light_eps, 1)
                pool.wait_ge(light_eps, l + 1)
                g.tensor_tensor(l_rstd[:], l_var_eps[:], minus_half[:, 0:1], ALU.pow).then_inc(light_rstd, 1)

            def light(q, u):
                if u == 0:
                    light_at(q - 1, light_make_rstd)
                if u == 2:
                    light_at(q + 1, gather_light)

            def make_rstd(t, q, u):
                nt, rows = pair_shape(t)
                b = u % 2
                wait(pool, mv_made, 2 * t + 2)
                wait(pool, shift_made, t - 1)
                wait(pool, normed, t - 1)
                pool.sem_inc(gate, 1)
                g.tensor_scalar(var_eps[0:rows, b, 0:nt], mv[0:rows, b, 0:nt, 1], EPS, None, ALU.add
                                ).then_inc(eps_added, 1)
                pool.wait_ge(eps_added, t + 1)
                g.tensor_tensor(rstd[0:rows, b, 0:nt], var_eps[0:rows, b, 0:nt], minus_half[0:rows, 0:nt], ALU.pow
                                ).then_inc(rstd_made, 1)

            gather_light(0)
            single(0, gather_cor)
            single(1, gather_cor)

            def serve(t, q, u):
                shifted(t, q, u, 2, NP, gather_cor)
                shifted(t, q, u, -2, NP, make_rstd)
                light(q, u)
            steps(pool, NP, serve)
            single(NP - 2, make_rstd)
            single(NP - 1, make_rstd)
            light_tail(light, NP, 4 * EARLY + 4)

        @block.tensor
        def _(pe):
            mm = nc.tensor.matmul
            pe.wait_ge(consts, 5)

            def three(ps, hi, lo, w_hi, w_lo, arriving=None):
                terms = [(a, w, k) for k in range(K) for a, w in ((hi, w_hi), (hi, w_lo), (lo, w_hi))]
                for n, (a, w, k) in enumerate(terms):
                    if arriving and n % 3 == 0:
                        pe.wait_ge(arriving, k + 1)
                    last = mm(ps, a[:, k], w[:, k], start=(n == 0), stop=(n == len(terms) - 1))
                return last

            def transpose_early(t, q, u):
                b, used = ring(q, u, 2)
                pe.wait_ge(early_x_in[b], 16 * (used + 1))
                wait(pe, early_copied, t - 1)
                for k in range(K):
                    last = nc.tensor.transpose(pT[b][:, 0, k * P:(k + 1) * P], e_x[b][:, k * P:(k + 1) * P], eye)
                last.then_inc(early_transposed, 1)

            def early_tile(t, q, u):
                shifted(t, q, u, 1, EARLY, transpose_early)
                b = u % 2
                wait(pe, early_hi, t + 1)
                wait(pe, early_lo, t + 1)
                wait(pe, early_kept, t - 1)
                three(pH[0][:, b, :], x_hi[b][:, 0], x_lo[b][:, 0], ws_hi, ws_lo,
                      ws_split if fixed(t) and t == 0 else None).then_inc(early_done, 1)
            single(0, transpose_early)
            peeled(0, 8, early_tile)
            looped(pe, 2, MERGE_ROUND, early_tile)
            pe.wait_ge(rows_moved, 1)
            for a in range(2):
                bank = pH[1][:, a, :]
                for c in range(CH):
                    mm(bank[:, c * P:(c + 1) * P], rowed_f[:, a * CH + c, P:2 * P], eye, start=(c == 0), stop=False)
                for c in range(CH):
                    lo = 1 if c == 0 else 0
                    last = mm(bank[:, c * P - 1 + lo:(c + 1) * P - 1], rowed_f[:, a * CH + c, 0:P],
                              eye[:, lo:P], start=False, stop=(c == CH - 1))
            last.then_inc(merged, 1)
            looped(pe, MERGE_ROUND, FIND_ROUND, early_tile)
            pe.wait_ge(dst_found, 1)
            nc.tensor.transpose(t_dst_ps, dst_f[:, 1:1 + ET], eye)
            mm(t_before_ps, dst_f[:, 0:ET], eye[:, P - 1:P], start=True, stop=True).then_inc(t_ready, 1)
            pe.wait_ge(upto_ready, 1)
            mm(before_ps, eye3[:, P - 1:2 * P - 1], upto[:, 1:1 + NTILES], start=True, stop=False)
            mm(before_ps, eye3[:, 2 * P - 1:3 * P - 1], upto[:, 0:NTILES], start=False, stop=True
               ).then_inc(before_ready, 1)
            single(4 * FIND_ROUND, early_tile)
            pe.wait_ge(t_scanned, 1)
            mm(ends_ps[:, 0:ET], t_run[0:ET, P - 1:P], eye[0:ET, 0:ET], start=True, stop=True)
            mm(ends_ps[:, ET:2 * ET], t_whole[0:ET, P - 1:P], eye[0:ET, 0:ET], start=True, stop=True
               ).then_inc(ends_ready, 1)
            single(4 * FIND_ROUND + 1, early_tile)
            pe.wait_ge(carry_ready, 1)
            mm(carry_ps, row_ends[0:1, 2, 0:ET], ones[0:1, 0:1], start=True, stop=True
               ).then_inc(carry_col, 1)
            peeled(4 * FIND_ROUND + 2, 4 * FIND_ROUND + 4, early_tile)
            pe.wait_ge(t_deg, 1)
            nc.tensor.transpose(rdeg_in_ps, t_rdeg[0:ET, :], eye[0:ET, 0:ET]).then_inc(rdeg_ps, 1)
            looped(pe, FIND_ROUND + 1, EARLY // 4 - 1, early_tile)

            def combine(t, q, u):
                b = u % 2
                wait(pe, sames_made, 2 * t + 2)
                wait(pe, diff_made, t + 1)
                if fixed(t) and t < 2:
                    pe.wait_ge(early_copied, EARLY - 1 + t)
                wait(pe, sums_made, t - 1)
                for k in range(K):
                    last = mm(pT[b][:, 0, k * P:(k + 1) * P], diff[b][:, k * P:(k + 1) * P], same[b][:],
                              start=True, stop=True)
                last.then_inc(summed, 1)

            peeled(EARLY - 4, EARLY - 1, early_tile)
            single(0, combine)
            single(EARLY - 1, early_tile)
            pe.wait_ge(rdeg_ready, 1)
            pe.wait_ge(early_kept, EARLY - 1)
            pe.wait_ge(wl_split, K)

            def transpose_x(t, q, u):
                nt, rows = pair_shape(t)
                b, used = ring(q, u, 4)
                pe.wait_ge(x_in[b], 16 * (used + 1))
                if fixed(t) and t < 2:
                    pe.wait_ge(sums_made, ET - 1 + t)
                wait(pe, lo_made, t - 1)
                for a in range(nt):
                    for k in range(K):
                        last = nc.tensor.transpose(pT[u % 2][:, a, k * P:k * P + rows],
                                                   X[0:rows, b, a, k * P:(k + 1) * P], eye[0:rows, 0:rows])
                last.then_inc(transposed, 1)

            def edge_tile(t, q, u):
                shifted(t, q, u, 1, ET, combine)
                if fixed(t) and t == ET - 1:
                    single(0, transpose_x)
                b = u % 2
                wait(pe, s_hi_made, t + 1)
                wait(pe, s_lo_made, t + 1)
                wait(pe, c_made, t - 1)
                three(pH[b][:, 0, :], s_hi[b], s_lo[b], wl_hi, wl_lo).then_inc(c_product, 1)
            steps(pe, ET, edge_tile)

            pe.wait_ge(early_kept, EARLY)

            def node_pair(t, q, u):
                shifted(t, q, u, 1, NP, transpose_x)
                nt, rows = pair_shape(t)
                b = u % 2
                wait(pe, hi_made, t + 1)
                wait(pe, lo_made, t + 1)
                if fixed(t) and t < 2:
                    pe.wait_ge(c_made, ET - 1 + t)
                wait(pe, z_made, t - 1)
                for a in range(nt):
                    last = three(pH[b][0:rows, a, :], x_hi[b][:, a, :, 0:rows], x_lo[b][:, a, :, 0:rows],
                                 ws_hi, ws_lo)
                last.then_inc(product, 1)
            steps(pe, NP, node_pair)

        @block.scalar
        def _(act):
            a_ = nc.scalar.activation
            act.wait_ge(pads_zero, 2)
            for tile, first in ((e_dst, 0), (e_next, 1)):
                act.dma_start(tile[:, 0:CH - 1], dst[first:first + FULL * P].rearrange("(c p j) -> p c j", p=P, j=P)
                             ).then_inc(edges_in, 16)
                rows = EDGE_ROWS - FULL
                act.dma_start(tile[0:rows, CH - 1], dst[first + FULL * P:first + EDGE_ROWS * P]
                             .rearrange("(p j) -> p j", j=P)).then_inc(edges_in, 16)
                tail = EDGE_TAIL - first
                act.dma_start(tile[rows:rows + 1, CH - 1, 0:tail], dst[first + EDGE_ROWS * P:E]
                             .rearrange("(p j) -> p j", p=1)).then_inc(edges_in, 16)
            act.preload_act_table_set("silu_and_others")

            def round_early(t, q, u):
                b = u % 2
                wait(act, early_transposed, t + 1)
                wait(act, early_done, t - 1)
                a_(x_hi[b][:, 0], pT[b][:, 0, :].rearrange("p (k r) -> p k r", k=K), ACT.Copy).then_inc(early_hi, 1)
                wait(act, early_lo, t - 1)
                a_(e_t[b][:], pT[b][:, 0, :], ACT.Copy).then_inc(early_copied, 1)

            def keep_early(t, q, u):
                b, used = ring(q, u, 2)
                wait(act, early_done, t + 1)
                wait(act, early_stored[b], 16 * used)
                a_(e_out[b][:], pH[0][:, b, :], ACT.Copy).then_inc(early_kept, 1)

            def early_tile(t, q, u):
                shifted(t, q, u, 1, EARLY, round_early)
                shifted(t, q, u, -1, EARLY, keep_early)
            single(0, round_early)
            for k in range(K):
                act.wait_ge(w_summed, k + 1)
                a_(ws_hi[:, k], w_sum[:, k], ACT.Copy).then_inc(ws_rounded, 1)
            single(0, early_tile)
            a_(wl_hi[:], wl_raw[:], ACT.Copy).then_inc(wl_rounded, 1)
            peeled(1, 8, early_tile)
            looped(act, 2, EARLY // 4 - 1, early_tile)

            def round_sums(t, q, u):
                b = u % 2
                wait(act, sums_made, t + 1)
                wait(act, c_product, t - 1)
                a_(s_hi[b][:], sums[:, b], ACT.Copy).then_inc(s_hi_made, 1)

            def reset_cor(t, q, u):
                wait(act, z_made, t - 3)
                a_(cor[u][:], bias_rows[:].rearrange("p (a n) -> p a n", a=1).to_broadcast([P, 2, D]), ACT.Copy
                   ).then_inc(cor_reset, 1)

            def reset_light(l):
                wait(act, light_z, l)
                a_(l_cor[:], bias_rows[:], ACT.Copy).then_inc(light_reset, 1)

            peeled(EARLY - 4, EARLY, early_tile)
            single(0, round_sums)
            single(EARLY - 1, keep_early)
            act.wait_ge(bias_in, 16)
            act.wait_ge(idx_ready, 1)
            act.wait_ge(early_lo, EARLY)
            reset_light(0)
            single(0, reset_cor)
            single(1, reset_cor)

            def edge_tile(t, q, u):
                shifted(t, q, u, 1, ET, round_sums)
            steps(act, ET, edge_tile)

            def round_x(t, q, u):
                nt, rows = pair_shape(t)
                b = u % 2
                wait(act, transposed, t + 1)
                wait(act, product, t - 1)
                a_(x_hi[b][:, 0:nt, :, 0:rows],
                   pT[b][:, 0:nt].rearrange("p a (k r) -> p a k r", k=K)[:, :, :, 0:rows], ACT.Copy).then_inc(hi_made, 1)

            def normalise(t, q, u):
                nt, rows = pair_shape(t)
                b, used = ring(q, u, 2)
                wait(act, shift_made, t + 1)
                wait(act, stored[b], 16 * used)
                for a in range(nt):
                    last = a_(O[0:rows, b, a], Z[0:rows, u % 4, a], ACT.Identity, scale=rstd[0:rows, b, a:a + 1],
                              bias=shift[0:rows, b, a:a + 1])
                last.then_inc(normed, 1)

            def silu(t, q, u):
                nt, rows = pair_shape(t)
                b = u % 4
                wait(act, z_made, t + 1)
                a_(Z[0:rows, b, 0:nt], Z[0:rows, b, 0:nt], ACT.Silu).then_inc(silu_made, 1)

            def light_make_silu(l):
                wait(act, light_z, l + 1)
                a_(l_z[:], l_z[:], ACT.Silu).then_inc(light_silu, 1)

            def light_normalise(l):
                wait(act, light_shift, l + 1)
                wait(act, light_stored, 16 * l)
                a_(l_o[:], l_u[:], ACT.Identity, scale=l_rstd[:, 0:1], bias=l_shift[:, 0:1]).then_inc(light_normed, 1)

            def light(q, u):
                if u == 1:
                    light_at(q - 1, light_normalise)
                if u == 2:
                    light_at(q, light_make_silu)
                    light_at(q + 1, reset_light)

            single(0, round_x)

            def node_pair(t, q, u):
                shifted(t, q, u, 2, NP, reset_cor)
                shifted(t, q, u, 1, NP, round_x)
                shifted(t, q, u, -1, NP, silu)
                light(q, u)
                shifted(t, q, u, -3, NP, normalise)
            steps(act, NP, node_pair)
            single(NP - 3, normalise)
            single(NP - 1, silu)
            light_tail(light, NP, 4 * EARLY)
            single(NP - 2, normalise)
            single(NP - 1, normalise)
            light_tail(light, 4 * EARLY, 4 * EARLY + 4)

        @block.vector
        def _(dve):
            v = nc.vector
            done = [0]

            def then(ins):
                done[0] += 1
                ins.then_inc(dve_step, 1)
                dve.wait_ge(dve_step, done[0])

            def sum_weights(k):
                dve.wait_ge(weights_in[k], 32)
                v.tensor_tensor(w_sum[:, k], wl_raw[:, k], wr_raw[:, k], ALU.add).then_inc(w_summed, 1)
            sum_weights(0)
            for k in range(K):
                if k + 1 < K:
                    sum_weights(k + 1)
                dve.wait_ge(ws_rounded, k + 1)
                v.tensor_tensor(ws_lo[:, k], w_sum[:, k], ws_hi[:, k].bitcast(f32), ALU.subtract).then_inc(ws_split, 1)

            v.memset(rowed[0], 0)
            then(v.memset(rowed[1], 0))
            dve.wait_ge(edges_in, 96)
            dve.wait_ge(pos_made, 2)
            v.tensor_tensor(e_rank, e_pos, e_dst, ALU.subtract)
            v.tensor_tensor(e_loop, e_dst, e_next, ALU.not_equal)
            then(v.tensor_tensor(e_other, e_dst, e_next, ALU.is_equal))
            v.tensor_tensor(rowed[0][:, 0:CH, P:], e_dst, e_other, ALU.mult)
            then(v.tensor_tensor(rowed[0][:, CH:, P:], e_rank, e_loop, ALU.mult))

            def move_left(out_, in_, mask, k, step, lo, hi):
                then(v.tensor_scalar(mask[:, :, lo:hi], in_[:, :, lo:hi], 31 - k, 31,
                                     ALU.logical_shift_left, ALU.arith_shift_right))
                then(v.scalar_tensor_tensor(out_[:, :, lo:hi], mask[:, :, lo:hi], -1, in_[:, :, lo:hi],
                                            ALU.bitwise_xor, ALU.bitwise_and))
                to = max(lo - step, 0)
                then(v.copy_predicated(out_[:, :, to:hi - step], mask[:, :, to + step:hi], in_[:, :, to + step:hi]))

            for k in range(ROW_BITS):
                move_left(rowed[(k + 1) % 2], rowed[k % 2], row_mask, k, 1 << k, P - (1 << k) + 1, 2 * P)
            then(v.tensor_copy(rowed_f[:], rowed[ROW_BITS % 2]))
            dve.sem_inc(rows_moved, 1)
            dve.wait_ge(merged, 1)
            then(v.tensor_copy(col[0], pH[1][:]))
            for k in range(ROW_BITS, BITS):
                n = k - ROW_BITS
                move_left(col[(n + 1) % 2], col[n % 2], col_mask, k, 1 << n, 0, COLS)
            found = col[(BITS - ROW_BITS) % 2]
            v.tensor_copy(dst_c, found[:, 0, 0:ET]).then_inc(dst_ready, 1)
            v.memset(upto[:, 0:1], 0.0)
            v.tensor_copy(upto[:, 1:1 + NTILES], found[:, 1, 0:NTILES]).then_inc(upto_ready, 1)
            dve.wait_ge(dst_padded, 1)
            then(v.tensor_tensor(edge_idx[:, :, 0], dst_c, r_pos, ALU.add))
            v.tensor_scalar(edge_idx[:, :, 0], edge_idx[:, :, 0], E - 1.0, None, ALU.min)
            v.tensor_scalar(edge_idx[:, :, 1], dst_c, N - 1.0, None, ALU.min)
            then(v.tensor_copy(dst_f[:, 1:1 + ET], dst_c))
            dve.sem_inc(dst_found, 1)
            dve.wait_ge(consts, 5)
            dve.wait_ge(t_ready, 1)
            v.tensor_copy(t_dst[0:ET, 1:1 + P], t_dst_ps)
            then(v.tensor_copy(t_dst[0:ET, 0:1], t_before_ps))
            dve.sem_inc(list_made, 1)
            then(v.tensor_tensor(t_same[0:ET], t_dst[0:ET, 1:1 + P], t_dst[0:ET, 0:P], ALU.is_equal))
            v.tensor_tensor_scan(t_run[0:ET], t_same[0:ET], ones[0:ET, :], 0.0, ALU.mult, ALU.add)
            v.tensor_tensor_scan(t_whole[0:ET], t_same[0:ET], zeros[0:ET, :], 1.0, ALU.mult, ALU.add
                                 ).then_inc(t_scanned, 1)
            dve.wait_ge(before_ready, 1)
            then(v.tensor_tensor(none, upto[:, 1:1 + NTILES], before_ps, ALU.subtract))
            then(v.tensor_scalar(none, none, 0.0, float(SKIP), ALU.is_equal, ALU.mult))
            v.memset(node_idx[:, NTILES:NTILES + 1], SKIP)
            v.scalar_tensor_tensor(node_idx[:, 0:NTILES], upto[:, 1:1 + NTILES], -1.0, none, ALU.add, ALU.add
                                   ).then_inc(idx_ready, 1)
            dve.wait_ge(ends_ready, 1)
            v.memset(row_ends[0:1, 2, 0:1], 0.0)
            then(v.tensor_copy(row_ends[0:1, 0:2, 0:ET],
                               ends_ps.rearrange("p (a c) -> p a c", a=2)))
            v.tensor_tensor_scan(row_ends[0:1, 2, 1:ET], row_ends[0:1, 1, 0:ET - 1], row_ends[0:1, 0, 0:ET - 1], 0.0,
                                 ALU.mult, ALU.add).then_inc(carry_ready, 1)
            dve.wait_ge(carry_col, 1)
            then(v.scalar_tensor_tensor(t_count[0:ET], t_whole[0:ET], carry_ps, t_run[0:ET],
                                        ALU.mult, ALU.add))
            then(v.tensor_scalar(t_count[0:ET], t_count[0:ET], 1.0, None, ALU.add))
            v.reciprocal(t_rdeg[0:ET], t_count[0:ET]).then_inc(t_deg, 1)
            dve.wait_ge(rdeg_ps, 1)
            then(v.tensor_copy(rdeg[:], rdeg_in_ps))
            dve.sem_inc(rdeg_ready, 1)
            dve.wait_ge(bias_in, 16)

            def compare(t, q, u):
                b = u % 2
                r, used = ring(q, u, 4)
                dve.wait_ge(row_in[r], 16 * (used + 1))
                wait(dve, summed, t - 1)
                v.tensor_scalar(same[b][:], dst_row[:, r, 1:1 + P], dst_f[:, bass.ds(1 + t, 1)], None, ALU.is_equal
                                ).then_inc(sames_made, 1)
                v.tensor_scalar(goes_on[:, b], dst_row[:, r, 1:1 + P], dst_row[:, r, 0:1], None, ALU.is_equal
                                ).then_inc(sames_made, 1)
                dve.wait_ge(xs_in[r], 16 * (used + 1))
                dve.wait_ge(xd_in[r], 16 * (used + 1))
                v.tensor_tensor(diff[b][:], xs[r][:], xd[r][:], ALU.subtract).then_inc(diff_made, 1)

            def carry(t, q, u):
                b = u % 2
                wait(dve, summed, t + 1)
                wait(dve, sums_made, t)
                wait(dve, s_lo_made, t - 1)
                wait(dve, s_hi_made, t - 1)
                for k in range(K):
                    last = v.scalar_tensor_tensor(
                        sums[:, b, k], goes_on[:, b], zeros[:, 0:1] if fixed(t) and t == 0 else sums[:, 1 - b, k, P - 1:P],
                        pT[b][:, 0, k * P:(k + 1) * P], ALU.mult, ALU.add)
                last.then_inc(sums_made, 1)

            def split_sums(t, q, u):
                b = u % 2
                wait(dve, s_hi_made, t + 1)
                wait(dve, c_product, t - 1)
                v.tensor_tensor(s_lo[b][:], sums[:, b], s_hi[b][:].bitcast(f32), ALU.subtract).then_inc(s_lo_made, 1)

            def finish(t, q, u):
                b, used = ring(q, u, 2)
                wait(dve, c_product, t + 1)
                wait(dve, c_stored[b], 16 * used)
                v.scalar_tensor_tensor(c_out[:, b], pH[b][:, 0, :], rdeg[:, bass.ds(t, 1)], bias_rows[:],
                                       ALU.mult, ALU.add).then_inc(c_made, 1)

            single(0, compare)
            single(0, carry)
            single(1, compare)
            single(0, split_sums)

            def edge_tile(t, q, u):
                shifted(t, q, u, -1, ET, finish)
                shifted(t, q, u, 1, ET, carry)
                shifted(t, q, u, 2, ET, compare)
                shifted(t, q, u, 1, ET, split_sums)
            steps(dve, ET, edge_tile)

            def split_x(t, q, u):
                nt, rows = pair_shape(t)
                b = u % 2
                wait(dve, hi_made, t + 1)
                v.tensor_tensor(x_lo[b][:, 0:nt, :, 0:rows],
                                pT[b][:, 0:nt].rearrange("p a (k r) -> p a k r", k=K)[:, :, :, 0:rows],
                                x_hi[b][:, 0:nt, :, 0:rows].bitcast(f32), ALU.subtract).then_inc(lo_made, 1)

            def add_cor(t, q, u):
                nt, rows = pair_shape(t)
                b, used = ring(q, u, 4)
                wait(dve, product, t + 1)
                if nt == 2:
                    dve.wait_ge(cor_in[b], 32 * (used + 1))
                else:
                    dve.wait_ge(cor_in[b], 32 * used + 16)
                wait(dve, normed, t - 3)
                v.tensor_tensor(Z[0:rows, b, 0:nt], pH[u % 2][0:rows, 0:nt], cor[b][0:rows, 0:nt], ALU.add
                                ).then_inc(z_made, 1)

            def residual(t, q, u):
                nt, rows = pair_shape(t)
                b = u % 4
                wait(dve, silu_made, t + 1)
                v.tensor_tensor(Z[0:rows, b, 0:nt], Z[0:rows, b, 0:nt], X[0:rows, b, 0:nt], ALU.add
                                ).then_inc(u_made, 1)

            def moments(t, q, u):
                nt, rows = pair_shape(t)
                wait(dve, u_made, t + 1)
                wait(dve, rstd_made, t - 1)
                for a in range(nt):
                    v.bn_stats(stats[0:rows, u % 2, a], Z[0:rows, u % 4, a]).then_inc(stats_made, 1)
                wait(dve, stats_made, 2 * t + nt)
                dve.sem_inc(dve_gate, 1)
                for a in range(nt):
                    v.bn_aggr(mv[0:rows, u % 2, a], stats[0:rows, u % 2, a]).then_inc(mv_made, 3 - nt)

            def make_shift(t, q, u):
                nt, rows = pair_shape(t)
                b = u % 2
                wait(dve, rstd_made, t + 1)
                wait(dve, normed, t - 1)
                v.scalar_tensor_tensor(shift[0:rows, b, 0:nt], mv[0:rows, b, 0:nt, 0], -1.0, rstd[0:rows, b, 0:nt],
                                       ALU.mult, ALU.mult).then_inc(shift_made, 1)

            def light_add(l):
                dve.wait_ge(light_in, 32 * (l + 1))
                dve.wait_ge(light_cor_in, 16 * (l + 1))
                v.tensor_tensor(l_z[:], l_h[:], l_cor[:], ALU.add).then_inc(light_z, 1)

            def light_residual(l):
                wait(dve, light_silu, l + 1)
                wait(dve, light_normed, l)
                v.tensor_tensor(l_u[:], l_z[:], l_x[:], ALU.add).then_inc(light_u, 1)

            def light_moments(l):
                wait(dve, light_u, l + 1)
                wait(dve, light_rstd, l)
                v.bn_stats(l_stats[:], l_u[:]).then_inc(light_stats, 1)
                wait(dve, light_stats, l + 1)
                dve.sem_inc(dve_gate, 1)
                v.bn_aggr(l_mv[:], l_stats[:]).then_inc(light_mv, 1)

            def light_make_shift(l):
                wait(dve, light_rstd, l + 1)
                wait(dve, light_normed, l)
                v.scalar_tensor_tensor(l_shift[:], l_mv[:, 0:1], -1.0, l_rstd[:], ALU.mult, ALU.mult
                                       ).then_inc(light_shift, 1)

            def light(q, u):
                if u == 0:
                    light_at(q - 1, light_make_shift)
                if u == 1:
                    light_at(q, light_add)
                if u == 2:
                    light_at(q, light_residual)
                if u == 3:
                    light_at(q, light_moments)

            single(0, split_x)
            single(ET - 1, finish)

            def node_pair(t, q, u):
                shifted(t, q, u, -1, NP, add_cor)
                shifted(t, q, u, -2, NP, moments)
                shifted(t, q, u, 1, NP, split_x)
                shifted(t, q, u, -1, NP, residual)
                shifted(t, q, u, -2, NP, make_shift)
                light(q, u)
            steps(dve, NP, node_pair)
            single(NP - 1, add_cor)
            single(NP - 2, moments)
            single(NP - 1, residual)
            single(NP - 2, make_shift)
            single(NP - 1, moments)
            light_tail(light, NP, 4 * EARLY)
            single(NP - 1, make_shift)
            light_tail(light, 4 * EARLY, 4 * EARLY + 4)


_INS = ["x", "src", "dst", "L0_gnn_W_l", "L0_gnn_W_r", "L0_gnn_b"]


def kernel(**inputs):
    import numpy as _np
    import concourse.bacc as _bacc
    from concourse import mybir as _mybir
    from concourse.bass_utils import run_bass_kernel_spmd as _run

    nc = _bacc.Bacc("TRN2", target_bir_lowering=False, num_devices=1)
    arrays, args = {}, []
    for name in _INS:
        a = _np.ascontiguousarray(inputs[name])
        arrays[f"in_{name}"] = a
        args.append(nc.dram_tensor(f"in_{name}", a.shape, _mybir.dt.from_np(a.dtype), kind="ExternalInput").ap())
    shape = tuple(inputs["x"].shape)
    args.append(nc.dram_tensor("out_0", shape, _mybir.dt.float32, kind="ExternalOutput").ap())
    gnn_layer(nc, *args)
    r = _run(nc, [arrays], core_ids=[0])
    return r.results[0]["out_0"]
```
